# Optimizing a Trainium2 kernel written in Bass

```python
import numpy as np
import jax
import jax.numpy as jnp

def _softmax(x, axis=-1):
    return jax.nn.softmax(x, axis=axis)

def _gelu(x):
    return jax.nn.gelu(x, approximate=True)

def _silu(x):
    return jax.nn.silu(x)

def _sigmoid(x):
    return jax.nn.sigmoid(x)

def _layernorm(x, axis=-1, eps=1e-05):
    m = jnp.mean(x, axis=axis, keepdims=True)
    v = jnp.var(x, axis=axis, keepdims=True)
    return (x - m) / jnp.sqrt(v + eps)

def _scatter_add(tgt, idx, src, axis=0):
    return tgt.at[idx].add(src)

def _segment_sum(src, seg, n):
    return jax.ops.segment_sum(src, seg, n)
kernel_name = 'mk_decoder_preln_d1_seqx_r8_4354c8'

def setup_inputs(seed: int=0):
    np.random.seed(seed)
    _w = jnp.asarray

    def _rec_inputs():
        import jax
        import jax.numpy as jnp
        _rk = jax.random.key(seed)
        x = 7.22e-05 + 1 * jax.random.normal(jax.random.fold_in(_rk, 1), (4, 256, 256), jnp.float32)
        _lenS = 256 - jax.random.randint(jax.random.fold_in(_rk, 7), (4,), 0, max(1, 256 // 4) + 1, jnp.int32)
        _lenS2 = 256 - jax.random.randint(jax.random.fold_in(_rk, 8), (4,), 0, max(1, 256 // 4) + 1, jnp.int32)
        _ctx_1024P = jax.random.normal(jax.random.fold_in(_rk, 11), (4, 16, 128), jnp.float32)
        _ctx_1024c = jax.random.dirichlet(jax.random.fold_in(_rk, 511), 0.3 * jnp.ones((16,), jnp.float32), (4, 256))
        _ctx_1024t = jnp.einsum('bsk,bkd->bsd', _ctx_1024c, _ctx_1024P)
        _ctx_1024t = _ctx_1024t * jax.lax.rsqrt(jnp.mean(jnp.square(_ctx_1024t)) + 1e-12) * 0.953939
        ctx_1024 = 2.81802e-05 + 1.00001 * (_ctx_1024t + 0.3 * jax.random.normal(jax.random.fold_in(_rk, 611), (4, 256, 128), jnp.float32))
        return (x, ctx_1024)
    x, ctx_1024 = _rec_inputs()

    def _L0_attn_setup():
        import jax, jax.numpy as jnp
        import numpy as np
        NUM_HEADS = 16
        ROPE_BASE = 10000.0

        def build_rope_cache(seq_len, n_elem):
            theta = 1.0 / ROPE_BASE ** (jnp.arange(0, n_elem, 2, dtype=jnp.float32) / n_elem)
            idx_theta = jnp.outer(jnp.arange(seq_len, dtype=jnp.float32), theta)
            return jnp.stack([jnp.cos(idx_theta), jnp.sin(idx_theta)], axis=-1)

        def apply_rope(x, rope):
            B, H, T, D = x.shape
            xt = x.transpose(0, 2, 1, 3)
            xs = xt.reshape(B, T, H, D // 2, 2)
            rc = rope[:T].reshape(1, T, 1, D // 2, 2)
            cos, sin = (rc[..., 0], rc[..., 1])
            x0, x1 = (xs[..., 0], xs[..., 1])
            out = jnp.stack([x0 * cos - x1 * sin, x1 * cos + x0 * sin], axis=-1)
            return out.reshape(B, T, H, D).transpose(0, 2, 1, 3)
        key = jax.random.key(seed)
        k1, k2, k3 = jax.random.split(key, 3)
        B, T, C = (2, 256, 256)
        x = jax.random.normal(k1, (B, T, C), dtype=jnp.float32)
        w_atten = jax.random.normal(k2, (3 * C, C), dtype=jnp.float32) * (1.0 / np.sqrt(C))
        w_proj = jax.random.normal(k3, (C, C), dtype=jnp.float32) * (1.0 / np.sqrt(C))
        return {'x': x, 'w_atten': w_atten, 'w_proj': w_proj}
    _L0_attn_all = _L0_attn_setup()
    _L0_attn_in = {k: v for k, v in _L0_attn_all.items() if k in ('w_atten', 'w_proj')}
    del _L0_attn_all

    def _L0_xattn_setup():
        import jax, jax.numpy as jnp
        import numpy as np
        key = jax.random.key(seed)
        ks = jax.random.split(key, 6)
        B, L, N, C, D = (8, 64, 256, 128, 128)
        return {'teacher_logits': jax.random.normal(ks[0], (B, L, N), dtype=jnp.float32), 'teacher_features': jax.random.normal(ks[1], (B, N, C), dtype=jnp.float32), 'Wq': jax.random.normal(ks[2], (D, C), dtype=jnp.float32) * (1.0 / np.sqrt(C)), 'bq': jnp.zeros((D,), dtype=jnp.float32), 'Wk': jax.random.normal(ks[3], (D, C), dtype=jnp.float32) * (1.0 / np.sqrt(C)), 'bk': jnp.zeros((D,), dtype=jnp.float32)}
    _L0_xattn_all = _L0_xattn_setup()
    _L0_xattn_in = {k: v for k, v in _L0_xattn_all.items() if k in ('Wq', 'bq', 'Wk', 'bk')}
    del _L0_xattn_all

    def _L0_ffn_setup():
        import jax, jax.numpy as jnp
        import numpy as np
        D_MODEL = 256
        D_EXPERT = 1024
        EPS = 1e-08

        def ternary_quant(w):
            scale = jnp.mean(jnp.abs(w)) + EPS
            q = jnp.clip(jnp.round(w / scale), -1.0, 1.0) * scale
            return w + jax.lax.stop_gradient(q - w)
        key = jax.random.key(seed)
        k_x, k_up, k_gate, k_down = jax.random.split(key, 4)
        std_in = 1.0 / np.sqrt(D_MODEL)
        std_exp = 1.0 / np.sqrt(D_EXPERT)
        return {'x': jax.random.normal(k_x, (4, 256, D_MODEL), dtype=jnp.float32), 'W_up': jax.random.normal(k_up, (D_EXPERT, D_MODEL), dtype=jnp.float32) * std_in, 'W_gate': jax.random.normal(k_gate, (D_EXPERT, D_MODEL), dtype=jnp.float32) * std_in, 'W_down': jax.random.normal(k_down, (D_MODEL, D_EXPERT), dtype=jnp.float32) * std_exp}
    _L0_ffn_all = _L0_ffn_setup()
    _L0_ffn_in = {k: v for k, v in _L0_ffn_all.items() if k in ('W_up', 'W_gate', 'W_down')}
    del _L0_ffn_all
    return {'x': x, 'ctx_1024': ctx_1024, 'L0_attn_w_atten': _L0_attn_in['w_atten'], 'L0_attn_w_proj': _L0_attn_in['w_proj'], 'L0_xattn_Wq': _L0_xattn_in['Wq'], 'L0_xattn_bq': _L0_xattn_in['bq'], 'L0_xattn_Wk': _L0_xattn_in['Wk'], 'L0_xattn_bk': _L0_xattn_in['bk'], 'L0_ffn_W_up': _L0_ffn_in['W_up'], 'L0_ffn_W_gate': _L0_ffn_in['W_gate'], 'L0_ffn_W_down': _L0_ffn_in['W_down']}

def reference(x, ctx_1024, L0_attn_w_atten, L0_attn_w_proj, L0_xattn_Wq, L0_xattn_bq, L0_xattn_Wk, L0_xattn_bk, L0_ffn_W_up, L0_ffn_W_gate, L0_ffn_W_down):
    import jax
    import jax.numpy as jnp

    def _L0_attn_ref(x, w_atten, w_proj):
        import jax, jax.numpy as jnp
        import numpy as np
        NUM_HEADS = 16
        ROPE_BASE = 10000.0

        def build_rope_cache(seq_len, n_elem):
            theta = 1.0 / ROPE_BASE ** (jnp.arange(0, n_elem, 2, dtype=jnp.float32) / n_elem)
            idx_theta = jnp.outer(jnp.arange(seq_len, dtype=jnp.float32), theta)
            return jnp.stack([jnp.cos(idx_theta), jnp.sin(idx_theta)], axis=-1)

        def apply_rope(x, rope):
            B, H, T, D = x.shape
            xt = x.transpose(0, 2, 1, 3)
            xs = xt.reshape(B, T, H, D // 2, 2)
            rc = rope[:T].reshape(1, T, 1, D // 2, 2)
            cos, sin = (rc[..., 0], rc[..., 1])
            x0, x1 = (xs[..., 0], xs[..., 1])
            out = jnp.stack([x0 * cos - x1 * sin, x1 * cos + x0 * sin], axis=-1)
            return out.reshape(B, T, H, D).transpose(0, 2, 1, 3)
        B, T, C = x.shape
        H = NUM_HEADS
        D = C // H
        qkv = x @ w_atten.T
        q, k, v = jnp.split(qkv, 3, axis=2)
        q = q.reshape(B, T, H, D).transpose(0, 2, 1, 3)
        k = k.reshape(B, T, H, D).transpose(0, 2, 1, 3)
        v = v.reshape(B, T, H, D).transpose(0, 2, 1, 3)
        rope = build_rope_cache(T, D)
        q = apply_rope(q, rope)
        k = apply_rope(k, rope)
        att = jnp.einsum('bhqd,bhkd->bhqk', q, k) * (1.0 / jnp.sqrt(jnp.float32(D)))
        causal = jnp.tril(jnp.ones((T, T), dtype=bool))
        att = jnp.where(causal[None, None], att, jnp.float32(-jnp.inf))
        att = jax.nn.softmax(att, axis=-1)
        y = jnp.einsum('bhqk,bhkd->bhqd', att, v)
        y = y.transpose(0, 2, 1, 3).reshape(B, T, C)
        return y @ w_proj.T

    def _L0_xattn_ref(teacher_logits, teacher_features, Wq, bq, Wk, bk):
        import jax, jax.numpy as jnp
        import numpy as np
        query = jnp.einsum('bnc,dc->bnd', teacher_features, Wq) + bq
        key = jnp.einsum('bnc,dc->bnd', teacher_features, Wk) + bk
        energy = jnp.einsum('bnd,bmd->bnm', query, key)
        attention = jax.nn.softmax(energy, axis=-1)
        x_m = jnp.einsum('bln,bmn->blm', teacher_logits, attention)
        return x_m

    def _L0_ffn_ref(x, W_up, W_gate, W_down):
        import jax, jax.numpy as jnp
        import numpy as np
        D_MODEL = 256
        D_EXPERT = 1024
        EPS = 1e-08

        def ternary_quant(w):
            scale = jnp.mean(jnp.abs(w)) + EPS
            q = jnp.clip(jnp.round(w / scale), -1.0, 1.0) * scale
            return w + jax.lax.stop_gradient(q - w)
        wu = ternary_quant(W_up)
        wg = ternary_quant(W_gate)
        wd = ternary_quant(W_down)
        up = jnp.einsum('bsd,ed->bse', x, wu)
        gate = jnp.einsum('bsd,ed->bse', x, wg)
        hidden = jax.nn.silu(up) * gate
        return jnp.einsum('bse,de->bsd', hidden, wd)
    x = x + _L0_attn_ref(_layernorm(x, axis=-1), L0_attn_w_atten, L0_attn_w_proj)
    x = x + _L0_xattn_ref(_layernorm(x, axis=-1), ctx_1024, L0_xattn_Wq, L0_xattn_bq, L0_xattn_Wk, L0_xattn_bk)
    x = x + _L0_ffn_ref(_layernorm(x, axis=-1), L0_ffn_W_up, L0_ffn_W_gate, L0_ffn_W_down)
    return x

_drawn_inputs = setup_inputs


def setup_inputs(seed=0):
    import zlib

    import numpy as np

    out = dict(_drawn_inputs(seed))
    spreads = {'L0_xattn_bq': (0.0, 0.1), 'L0_xattn_bk': (0.0, 0.1)}
    factors = {}
    for name, (base, spread) in spreads.items():
        noise = np.random.default_rng([zlib.crc32(name.encode()), seed]).standard_normal(out[name].shape)
        drawn = base * np.exp(spread * noise) if base else spread * noise
        out[name] = jnp.asarray(drawn.astype(out[name].dtype))
    for name, factor in factors.items():
        out[name] = (out[name] * factor).astype(out[name].dtype)
    return out
```

```python
from contextlib import ExitStack

import numpy as np

import concourse.bass as bass
from concourse import mybir

F32 = mybir.dt.float32
F32R = mybir.dt.float32r
F16 = mybir.dt.float16
BF16 = mybir.dt.bfloat16
ALU = mybir.AluOpType
ACT = mybir.ActivationFunctionType
AX = mybir.AxisListType

P = 128
B = 4
T = 256
C = 256
H = 16
D = C // H
E = 1024
DX = 128
TT = T // P
CT = C // P
ET = E // P
G = H // 4
TERMS = 4
ROWS = TERMS * D
MROW = 96
ONES_ROW = 2
EPS_LN = 1e-5
EPS_Q = 1e-8
MASKED = -1e30
SQ_STEPS = TT * 2 + H // 2
ST_STEPS = 3 * G


def merged(*streams):
    at = [((n + 0.5) / len(s), k, step) for k, s in enumerate(streams) for n, step in enumerate(s)]
    return [step for _, _, step in sorted(at, key=lambda x: x[:2])]


def steps():

    def head(b):
        return [("ln_stats1", b, 0), ("ln_apply1", b, 0), ("ctx_qk", b, 0), ("ln_turn1", b, 0),
                ("qk", b, 0), ("qk", b, 1), ("ctx_scores", b, 0), ("v", b, 0), ("pack", b, 0), ("pack", b, 1),
                ("ctx_turn", b, 0)]

    def middle(b):
        out = [("sq", b, j) for j in range(SQ_STEPS)] + [("max_rows", b, 0)]
        for g in range(G):
            out += [("st", b, 3 * g + u) for u in range(3)]
            if g:
                out.append(("pv", b, g - 1))
        return out + [("pv", b, G - 1)]

    def tail(b):
        out = [("y_turn", b, 0), ("y_turn", b, 1), ("yn_turn", b, 0), ("proj", b, 0)]
        out += [("ln_stats2", b, 0), ("ln_apply2", b, 0), ("ln_turn2", b, 0), ("cross", b, 0)]
        out += [("ln_stats3", b, 0), ("ln_apply3", b, 0), ("ln_turn3", b, 0)]
        out += [("up_gate", b, m) for m in range(ET)] + [("down", b, 0)]
        return out

    order = [("setup", 0, 0)] + head(0)
    for i in range(B + 1):
        streams = []
        if i < B:
            streams.append(middle(i))
        if i + 1 < B:
            streams.append(head(i + 1))
        if i > 0:
            streams.append(tail(i - 1))
        if i == 0:
            streams.append([("ternary", 0, k) for k in range(3)])
        order += merged(*streams)
    return order


def decoder_kernel(nc, x_in, ctxT_in, wqkvT_in, wpT_in, wctxT_in, bctx_in, wupT_in, wgateT_in, wdownT_in,
                   consts_in, out):
    ORDER = steps()

    with ExitStack() as ctx:
        def sb(name, shape, dt=F32):
            return ctx.enter_context(nc.sbuf_tensor(name, shape, dt))

        def psum(name, shape):
            return ctx.enter_context(nc.psum_tensor(name, shape, F32))

        def sem(name):
            return ctx.enter_context(nc.semaphore(name))

        sq_bank = [psum(f"sq_bank{i}", [P, 512]) for i in range(2)]
        st_bank = [psum(f"st_bank{i}", [P, 512]) for i in range(2)]
        pv_bank = psum("pv_bank", [P, 512])
        misc_bank = psum("misc_bank", [P, 512])
        dense_bank = [psum(f"dense_bank{i}", [P, 512]) for i in range(2)]

        x = sb("x", [P, B, TT, C])
        w_qkv = sb("w_qkv", [P, CT, 3 * C])
        w_qkv_hi = sb("w_qkv_hi", [P, CT, 3 * C], F32R)
        w_qkv_lo = sb("w_qkv_lo", [P, CT, 3 * C], F32R)
        w_proj = sb("w_proj", [P, CT, C])
        w_ctx = sb("w_ctx", [P, 2, DX])
        b_ctx = sb("b_ctx", [P, 2])
        w_ffn = [sb(f"w_ffn{k}", [P, 2048]) for k in range(3)]
        w_tern = [sb(f"w_tern{k}", [P, 2048], F16) for k in range(3)]
        tern_neg = sb("tern_neg", [P, 2048], F16)
        abs_sum = sb("abs_sum", [P, 3])
        scales = sb("scales", [P, 3])
        half_pos = sb("half_pos", [P, 3])
        half_neg = sb("half_neg", [P, 3])
        out_scale = sb("out_scale", [P, 2])
        consts = sb("consts", [P, P + 2 * T])
        ident = consts[:, 0:P]
        cos_t, sin_t = consts[:, P:P + T], consts[:, P + T:P + 2 * T]
        ident16 = sb("ident16", [P, P], BF16)
        mask16 = sb("mask16", [P, 4, P], BF16)
        ones = sb("ones", [P, P])
        neg_half = sb("neg_half", [P, TT])

        stats = sb("stats", [P, TT, 6])
        mean_var = sb("mean_var", [P, TT, 2])
        var_eps = sb("var_eps", [P, TT])
        rstd = sb("rstd", [P, TT])
        xn = sb("xn", [P, TT, C])
        xT_hi = sb("xT_hi", [P, CT, T], F32R)
        xT_lo = sb("xT_lo", [P, CT, T], F32R)
        x2T = sb("x2T", [P, CT, T])
        x3T = sb("x3T", [P, 2, CT, T], F16)

        swapped = [sb(f"swapped{s}", [P, CT, T]) for s in range(2)]
        turned = [sb(f"turned{s}", [P, CT, T]) for s in range(2)]
        parts = [sb(f"parts{s}", [P, 2, CT, T], F32R) for s in range(2)]
        pack = [[sb(f"pack{s}{i}", [P, H, T], F32R) for i in range(2)] for s in range(2)]
        v_aug = [sb(f"v_aug{i}", [P, TT, H, 32]) for i in range(2)]
        neg_max = sb("neg_max", [P, TT, H])
        max_parts = sb("max_parts", [P, TT, 2, H], F32R)
        maxT = sb("maxT", [32, T])
        probs = [sb(f"probs{i}", [P, 3, 512]) for i in range(2)]
        yT_raw = sb("yT_raw", [P, G, T])
        y_rec = sb("y_rec", [P, TT, H])
        yn = sb("yn", [P, TT, C])
        ynT = sb("ynT", [P, CT, T])

        ctxT = sb("ctxT", [P, B, T])
        ctx_qk = sb("ctx_qk", [P, 2, T])
        ctx_negmax = sb("ctx_negmax", [P, TT])
        ctx_sum = sb("ctx_sum", [P, TT])
        ctx_rec = sb("ctx_rec", [P, TT])
        ctx_exp = sb("ctx_exp", [P, TT, T])
        ctx_attn = sb("ctx_attn", [P, TT, T])
        attnT = [sb(f"attnT{i}", [P, CT, T]) for i in range(2)]

        spare = w_ffn[1][:].rearrange("p (n t) -> p n t", t=T)
        tanh_up = [spare[:, i] for i in range(2)]
        act_up = [spare[:, 2 + i] for i in range(2)]
        hidden = [spare[:, 4 + i] for i in range(2)]
        result = spare[:, 6:8]
        hid = w_ffn[0][:].bitcast(F16).rearrange("p (a m t) -> p a m t", a=2, m=ET)

        scratch = nc.dram_tensor("scratch", (2, B, 2, C, T), F32, kind="Internal").ap()

        x_loaded = [sem(f"x_loaded{b}") for b in range(B)]
        wqkv_loaded = sem("wqkv_loaded")
        consts_loaded = sem("consts_loaded")
        ctx_loaded = sem("ctx_loaded")
        wproj_loaded = sem("wproj_loaded")
        ffn_loaded = [sem(f"ffn_loaded{k}") for k in range(3)]
        ones_set = sem("ones_set")
        neg_half_set = sem("neg_half_set")
        ident16_made = sem("ident16_made")
        mask_filled = sem("mask_filled")
        mask_made = sem("mask_made")
        pack_rows_set = sem("pack_rows_set")
        v_ones_set = sem("v_ones_set")
        key_rows_set = sem("key_rows_set")
        w_hi_made = sem("w_hi_made")
        w_lo_made = sem("w_lo_made")
        abs_summed = sem("abs_summed")
        abs_total = sem("abs_total")
        scales_made = sem("scales_made")
        halves_made = sem("halves_made")
        out_scale_made = sem("out_scale_made")
        tern_neg_made = sem("tern_neg_made")
        tern_made = sem("tern_made")
        stats_made = [sem(f"stats_made{k}") for k in (1, 2, 3)]
        moments_made = [sem(f"moments_made{k}") for k in (1, 2, 3)]
        var_made = [sem(f"var_made{k}") for k in (1, 2, 3)]
        rstd_made = [sem(f"rstd_made{k}") for k in (1, 2, 3)]
        normed = [sem(f"normed{k}") for k in (1, 2, 3)]
        turned_ln = [sem(f"turned_ln{k}") for k in (1, 2, 3)]
        lnT_hi = [sem(f"lnT_hi{k}") for k in (1, 2, 3)]
        lnT_lo = [sem(f"lnT_lo{k}") for k in (1, 2, 3)]
        qk_projected = sem("qk_projected")
        qk_swapped = sem("qk_swapped")
        qk_cos = sem("qk_cos")
        qk_sin = sem("qk_sin")
        qk_rotated = sem("qk_rotated")
        qk_hi = sem("qk_hi")
        qk_lo = sem("qk_lo")
        scratch_written = [sem(f"scratch_written{s}") for s in range(2)]
        packed = [[sem(f"packed{s}{i}") for i in range(2)] for s in range(2)]
        v_projected = sem("v_projected")
        v_stored = sem("v_stored")
        sq_made = sem("sq_made")
        sq_maxed = sem("sq_maxed")
        max_hi = sem("max_hi")
        max_lo = sem("max_lo")
        max_turned = sem("max_turned")
        maxT_made = sem("maxT_made")
        max_placed = [sem(f"max_placed{i}") for i in range(2)]
        st_made = sem("st_made")
        exp_made = sem("exp_made")
        probs_masked = sem("probs_masked")
        pv_made = sem("pv_made")
        y_stored = sem("y_stored")
        y_turned = sem("y_turned")
        y_rec_made = sem("y_rec_made")
        y_normed = sem("y_normed")
        yn_turned = sem("yn_turned")
        ynT_stored = sem("ynT_stored")
        projected = sem("projected")
        x1_made = sem("x1_made")
        ctx_projected = sem("ctx_projected")
        ctx_qk_made = sem("ctx_qk_made")
        ctx_scored = sem("ctx_scored")
        ctx_maxed = sem("ctx_maxed")
        ctx_exped = sem("ctx_exped")
        ctx_rec_made = sem("ctx_rec_made")
        ctx_normed = sem("ctx_normed")
        ctx_turned = sem("ctx_turned")
        attnT_stored = sem("attnT_stored")
        crossed = sem("crossed")
        x2_made = sem("x2_made")
        up_gate_made = sem("up_gate_made")
        tanh_made = sem("tanh_made")
        act_made = sem("act_made")
        hidden_made = sem("hidden_made")
        hid_hi = sem("hid_hi")
        hid_lo = sem("hid_lo")
        down_made = sem("down_made")
        result_made = sem("result_made")
        stored = sem("stored")

        MISC = {
            "setup": lambda b, j: (scales_made, 1),
            "ln_turn1": lambda b, j: (lnT_lo[0], b + 1),
            "ln_turn2": lambda b, j: (lnT_hi[1], b + 1),
            "ln_turn3": lambda b, j: (lnT_lo[2], b + 1),
            "v": lambda b, j: (v_stored, b + 1),
            "max_rows": lambda b, j: (maxT_made, b + 1),
            "y_turn": lambda b, j: (y_normed, TT * b + j + 1),
            "yn_turn": lambda b, j: (ynT_stored, b + 1),
            "proj": lambda b, j: (x1_made, b + 1),
            "ctx_qk": lambda b, j: (ctx_qk_made, 2 * (b + 1)),
            "ctx_scores": lambda b, j: (ctx_exped, TT * (b + 1)),
            "ctx_turn": lambda b, j: (attnT_stored, b + 1),
            "cross": lambda b, j: (x2_made, b + 1),
            "ternary": None,
        }
        DENSE = {
            "qk": lambda b, j: (qk_cos, 2 * b + j + 1),
            "up_gate": lambda b, j: (hidden_made, ET * b + j + 1),
            "down": lambda b, j: (result_made, b + 1),
        }
        misc_before, dense_before, dense_at = {}, {}, {}
        last, users = None, []
        for step in ORDER:
            name, b, j = step
            if name == "ternary" and j > 0:
                continue
            if name in MISC and name != "setup":
                misc_before[step] = last
                last = (scales_made, 1) if name == "ternary" else MISC[name](b, j)
            if name in DENSE:
                dense_at[step] = len(users) % 2
                dense_before[step] = users[-2] if len(users) >= 2 else None
                users.append(DENSE[name](b, j))

        def free_misc(pe, step):
            if misc_before[step] is not None:
                pe.wait_ge(*misc_before[step])

        def free_dense(pe, step):
            if dense_before[step] is not None:
                pe.wait_ge(*dense_before[step])

        block = ctx.enter_context(nc.Block())

        @block.sync
        def _(sp):
            def load(dst, src, signal):
                sp.dma_start(dst, src).then_inc(signal, 16)

            x_v = x_in.rearrange("b (i p) c -> p b i c", p=P)
            out_v = out.rearrange("b (i p) c -> p b i c", p=P)
            load(x[:, 0], x_v[:, 0], x_loaded[0])
            load(w_qkv[:], wqkvT_in.rearrange("(k p) n -> p k n", p=P), wqkv_loaded)
            load(consts[:], consts_in, consts_loaded)
            load(w_ctx[:], wctxT_in.rearrange("a c d -> c a d"), ctx_loaded)
            load(b_ctx[:], bctx_in, ctx_loaded)
            load(ctxT[:], ctxT_in.rearrange("b c t -> c b t"), ctx_loaded)
            load(w_ffn[0][:].rearrange("p (k n) -> p k n", k=CT), wupT_in.rearrange("(k p) n -> p k n", p=P), ffn_loaded[0])
            load(w_ffn[1][:].rearrange("p (k n) -> p k n", k=CT), wgateT_in.rearrange("(k p) n -> p k n", p=P), ffn_loaded[1])
            load(w_ffn[2][:].rearrange("p (k n) -> p k n", k=ET), wdownT_in.rearrange("(k p) n -> p k n", p=P), ffn_loaded[2])
            load(x[:, 1], x_v[:, 1], x_loaded[1])
            load(w_proj[:], wpT_in.rearrange("(k p) n -> p k n", p=P), wproj_loaded)
            load(x[:, 2], x_v[:, 2], x_loaded[2])
            load(x[:, 3], x_v[:, 3], x_loaded[3])
            sp.wait_ge(pack_rows_set, 3)
            sp.wait_ge(key_rows_set, 1)
            for name, b, j in ORDER:
                if name == "pack":
                    s = j
                    sp.wait_ge(qk_hi, 2 * b + s + 1)
                    sp.wait_ge(qk_lo, 2 * b + s + 1)
                    sp.dma_start(scratch[s, b].rearrange("a (k p) t -> p a k t", p=P),
                                 parts[s][:].bitcast(F32)).then_inc(scratch_written[s], 16)
                    sp.wait_ge(scratch_written[s], 16 * (b + 1))
                    if b >= 2:
                        sp.wait_ge(st_made, ST_STEPS * (b - 1))
                    for t in range(TERMS):
                        part = t // 2 if s == 0 else t % 2
                        sp.dma_start(pack[s][b % 2][D * t:D * (t + 1), :, :].bitcast(F32),
                                     scratch[s, b, part].rearrange("(h d) t -> d h t", d=D)
                                     ).then_inc(packed[s][b % 2], 16)
                elif name == "max_rows":
                    sp.wait_ge(maxT_made, b + 1)
                    for a in range(2):
                        sp.dma_start(pack[0][b % 2][MROW + a:MROW + a + 1, :, :].bitcast(F32),
                                     maxT[H * a:H * (a + 1), :]).then_inc(max_placed[b % 2], 16)
                elif name == "down":
                    sp.wait_ge(result_made, b + 1)
                    sp.dma_start(out_v[:, b], result).then_inc(stored, 16)
            sp.wait_ge(stored, 16 * B)

        @block.gpsimd
        def _(pool):
            nc.gpsimd.memset(neg_half[:], -0.5).then_inc(neg_half_set, 1)
            nc.gpsimd.memset(mask16[:], MASKED).then_inc(mask_filled, 1)
            pool.wait_ge(mask_filled, 1)
            nc.gpsimd.affine_select(out=mask16[:], in_=mask16[:], compare_op=ALU.is_gt, fill=0.0, base=0,
                                    pattern=[[0, 4], [1, P]], channel_multiplier=-1).then_inc(mask_made, 1)
            pool.wait_ge(mask_made, 1)
            nc.gpsimd.memset(pack[0][0][64:P].bitcast(F32), 0.0).then_inc(pack_rows_set, 1)
            for n, i in enumerate(range(2)):
                pool.wait_ge(pack_rows_set if i == 0 else v_ones_set, 1)
                nc.gpsimd.memset(v_aug[i][:, :, :, D:32], 1.0).then_inc(v_ones_set, 1)
            pool.wait_ge(v_ones_set, 2)
            nc.gpsimd.memset(pack[0][1][64:P].bitcast(F32), 0.0).then_inc(pack_rows_set, 1)
            pool.wait_ge(pack_rows_set, 2)
            nc.gpsimd.memset(pack[1][1][64:P].bitcast(F32), 1.0).then_inc(pack_rows_set, 1)
            pool.wait_ge(pack_rows_set, 3)
            for name, b, j in ORDER:
                if name.startswith("ln_stats"):
                    k = int(name[-1]) - 1
                    pool.wait_ge(var_made[k], b + 1)
                    if b == 0 and k == 0:
                        pool.wait_ge(neg_half_set, 1)
                    nc.gpsimd.tensor_tensor(rstd[:], var_eps[:], neg_half[:], ALU.pow).then_inc(rstd_made[k], 1)
                elif name == "qk":
                    n = 2 * b + j
                    pool.wait_ge(qk_swapped, n + 1)
                    nc.gpsimd.tensor_tensor(swapped[j][:], swapped[j][:],
                                            sin_t.rearrange("p (k t) -> p k t", k=1).broadcast_to((P, CT, T)),
                                            ALU.mult).then_inc(qk_sin, 1)
                    pool.wait_ge(qk_sin, n + 1)
                    pool.wait_ge(qk_cos, n + 1)
                    nc.gpsimd.tensor_tensor(turned[j][:], turned[j][:], swapped[j][:], ALU.add).then_inc(qk_rotated, 1)
                elif name == "st" and j % 3 == 2:
                    n = G * b + j // 3
                    pr = probs[n % 2]
                    pool.wait_ge(exp_made, 3 * (n + 1))
                    for sel in (pr[:, 0:2, :].rearrange("p u (h q) -> p (u h) q", q=T)[:, :, 0:P],
                                pr[:, 2, :].rearrange("p (h q) -> p h q", q=P)):
                        nc.gpsimd.affine_select(out=sel, in_=sel, compare_op=ALU.is_ge, fill=0.0, base=0,
                                                pattern=[[0, 4], [1, P]], channel_multiplier=-1
                                                ).then_inc(probs_masked, 1)
                elif name == "up_gate" or name == "down":
                    m = (j if name == "up_gate" else ET) - 1
                    if m < 0:
                        continue
                    n = ET * b + m
                    pool.wait_ge(hid_hi, n + 1)
                    nc.gpsimd.tensor_tensor(hid[:, 1, m], hidden[n % 2], hid[:, 0, m], ALU.subtract
                                            ).then_inc(hid_lo, 1)

        @block.scalar
        def _(act):
            act.wait_ge(wqkv_loaded, 16)
            nc.scalar.activation(w_qkv_hi[:], w_qkv[:], ACT.Copy).then_inc(w_hi_made, 1)
            for name, b, j in ORDER:
                if name == "ternary":
                    if j == 0:
                        for k in range(3):
                            act.wait_ge(ffn_loaded[k], 16)
                            if k:
                                act.wait_ge(abs_summed, k)
                            nc.scalar.activation(tern_neg[:], w_ffn[k][:], ACT.Abs, accum_out=abs_sum[:, k:k + 1]
                                                 ).then_inc(abs_summed, 1)
                elif name == "ln_turn1":
                    act.wait_ge(turned_ln[0], b + 1)
                    if b:
                        act.wait_ge(v_projected, b)
                        act.wait_ge(qk_projected, 2 * b)
                        act.wait_ge(lnT_lo[0], b)
                    nc.scalar.activation(xT_hi[:], misc_bank[:].rearrange("p (k t) -> p k t", k=CT), ACT.Copy
                                         ).then_inc(lnT_hi[0], 1)
                elif name == "ln_turn2":
                    act.wait_ge(turned_ln[1], b + 1)
                    if b:
                        act.wait_ge(crossed, b)
                    nc.scalar.activation(x2T[:], misc_bank[:].rearrange("p (k t) -> p k t", k=CT), ACT.Copy
                                         ).then_inc(lnT_hi[1], 1)
                elif name == "ln_turn3":
                    act.wait_ge(turned_ln[2], b + 1)
                    if b:
                        act.wait_ge(up_gate_made, ET * b)
                        act.wait_ge(lnT_lo[2], b)
                    nc.scalar.activation(x3T[:, 0], misc_bank[:].rearrange("p (k t) -> p k t", k=CT), ACT.Copy
                                         ).then_inc(lnT_hi[2], 1)
                elif name == "qk":
                    n = 2 * b + j
                    act.wait_ge(qk_rotated, n + 1)
                    if b:
                        act.wait_ge(scratch_written[j], 16 * b)
                    nc.scalar.activation(parts[j][:, 0], turned[j][:], ACT.Copy).then_inc(qk_hi, 1)
                elif name == "v":
                    act.wait_ge(v_projected, b + 1)
                    act.wait_ge(v_ones_set, 2)
                    if b >= 2:
                        act.wait_ge(pv_made, G * (b - 1))
                    nc.scalar.activation(v_aug[b % 2][:, :, :, 0:D],
                                         misc_bank[:].rearrange("p (k h d) -> p k h d", k=TT, h=H), ACT.Copy
                                         ).then_inc(v_stored, 1)
                elif name == "max_rows":
                    act.wait_ge(max_turned, b + 1)
                    if b:
                        act.wait_ge(max_placed[(b - 1) % 2], 32 * ((b - 1) // 2 + 1))
                    nc.scalar.activation(maxT[:], misc_bank[0:32, 0:T], ACT.Copy).then_inc(maxT_made, 1)
                elif name == "st":
                    n = ST_STEPS * b + j
                    g = n // 3
                    act.wait_ge(st_made, n + 1)
                    if g >= 2:
                        act.wait_ge(pv_made, g - 1)
                    nc.scalar.activation(probs[g % 2][:, j % 3, :], st_bank[n % 2][:], ACT.Exp, scale=D ** -0.5
                                         ).then_inc(exp_made, 1)
                elif name == "pv" and j % 2 == 1:
                    act.wait_ge(pv_made, G * b + j + 1)
                    if b:
                        act.wait_ge(y_turned, TT * b)
                    nc.scalar.activation(yT_raw[:, j - 1:j + 1, :], pv_bank[:].rearrange("p (g t) -> p g t", g=2),
                                         ACT.Copy).then_inc(y_stored, 1)
                elif name == "yn_turn":
                    act.wait_ge(yn_turned, b + 1)
                    if b:
                        act.wait_ge(projected, b)
                    nc.scalar.activation(ynT[:], misc_bank[:].rearrange("p (k t) -> p k t", k=CT), ACT.Copy
                                         ).then_inc(ynT_stored, 1)
                elif name == "ctx_qk":
                    act.wait_ge(ctx_projected, b + 1)
                    act.wait_ge(ctx_loaded, 48)
                    if b:
                        act.wait_ge(ctx_scored, b)
                    for a in range(2):
                        nc.scalar.activation(ctx_qk[:, a], misc_bank[:, a * T:(a + 1) * T], ACT.Identity,
                                             bias=b_ctx[:, a:a + 1]).then_inc(ctx_qk_made, 1)
                elif name == "ctx_scores":
                    act.wait_ge(ctx_maxed, b + 1)
                    if b:
                        act.wait_ge(ctx_normed, TT * b)
                    for i in range(TT):
                        nc.scalar.activation(ctx_exp[:, i], misc_bank[:, i * T:(i + 1) * T], ACT.Exp,
                                             bias=ctx_negmax[:, i:i + 1], accum_out=ctx_sum[:, i:i + 1]
                                             ).then_inc(ctx_exped, 1)
                elif name == "ctx_turn":
                    act.wait_ge(ctx_turned, b + 1)
                    if b >= 2:
                        act.wait_ge(crossed, b - 1)
                    nc.scalar.activation(attnT[b % 2][:], misc_bank[:].rearrange("p (k t) -> p k t", k=CT), ACT.Copy
                                         ).then_inc(attnT_stored, 1)
                elif name == "up_gate" or name == "down":
                    if name == "up_gate":
                        n = ET * b + j
                        act.wait_ge(up_gate_made, n + 1)
                        act.wait_ge(halves_made, 2)
                        if n >= 2:
                            act.wait_ge(act_made, n - 1)
                        nc.scalar.activation(tanh_up[n % 2], dense_bank[dense_at[(name, b, j)]][:, 0:T], ACT.Tanh,
                                             scale=half_pos[:, 0:1]).then_inc(tanh_made, 1)
                    m = (j if name == "up_gate" else ET) - 1
                    if m >= 0:
                        n = ET * b + m
                        act.wait_ge(hidden_made, n + 1)
                        if b and m == 0:
                            act.wait_ge(down_made, b)
                        nc.scalar.activation(hid[:, 0, m], hidden[n % 2], ACT.Copy).then_inc(hid_hi, 1)

        @block.vector
        def _(dve):
            nc.vector.memset(ones[:], 1.0).then_inc(ones_set, 1)
            nc.vector.memset(pack[1][0][64:P].bitcast(F32), 1.0).then_inc(key_rows_set, 1)

            def layernorm_stats(k, b):
                if k == 0:
                    dve.wait_ge(x_loaded[b], 16)
                if k == 1:
                    dve.wait_ge(x1_made, b + 1)
                if k == 2:
                    dve.wait_ge(x2_made, b + 1)
                for i in range(TT):
                    nc.vector.bn_stats(stats[:, i], x[:, b, i]).then_inc(stats_made[k], 1)
                dve.wait_ge(stats_made[k], TT * (b + 1))
                for i in range(TT):
                    nc.vector.bn_aggr(mean_var[:, i], stats[:, i]).then_inc(moments_made[k], 1)
                dve.wait_ge(moments_made[k], TT * (b + 1))
                nc.vector.tensor_scalar(var_eps[:], mean_var[:, :, 1], EPS_LN, None, ALU.add).then_inc(var_made[k], 1)

            def layernorm_apply(k, b, before):
                dve.wait_ge(rstd_made[k], b + 1)
                if before is not None:
                    dve.wait_ge(*before)
                for i in range(TT):
                    nc.vector.tensor_scalar(xn[:, i], x[:, b, i], mean_var[:, i, 0:1], rstd[:, i:i + 1],
                                            ALU.subtract, ALU.mult).then_inc(normed[k], 1)

            lns = [(int(s[0][-1]) - 1, s[1]) for s in ORDER if s[0].startswith("ln_apply")]
            xn_before = {a: (turned_ln[z[0]], z[1] + 1) for z, a in zip(lns, lns[1:])}

            for name, b, j in ORDER:
                if name == "setup":
                    dve.wait_ge(consts_loaded, 16)
                    nc.vector.tensor_copy(ident16[:], ident).then_inc(ident16_made, 1)
                elif name == "ternary":
                    if j == 0:
                        dve.wait_ge(abs_total, 1)
                        nc.vector.tensor_scalar(scales[:], misc_bank[:, 0:3], 1.0 / (C * E), EPS_Q, ALU.mult, ALU.add
                                                ).then_inc(scales_made, 1)
                        dve.wait_ge(scales_made, 1)
                        nc.vector.tensor_scalar(half_pos[:], scales[:], 0.5, None, ALU.mult).then_inc(halves_made, 1)
                        nc.vector.tensor_scalar(half_neg[:], scales[:], -0.5, None, ALU.mult).then_inc(halves_made, 1)
                        nc.vector.tensor_tensor(out_scale[:, 0:1], scales[:, 0:1], scales[:, 1:2], ALU.mult
                                                ).then_inc(out_scale_made, 1)
                        dve.wait_ge(out_scale_made, 1)
                        nc.vector.tensor_scalar(out_scale[:, 1:2], out_scale[:, 0:1], scales[:, 2:3], 4.0, ALU.mult,
                                                ALU.mult).then_inc(out_scale_made, 1)
                        dve.wait_ge(halves_made, 2)
                        dve.wait_ge(abs_summed, 3)
                    if j:
                        dve.wait_ge(tern_made, j)
                    nc.vector.tensor_scalar(tern_neg[:], w_ffn[j][:], half_neg[:, j:j + 1], None, ALU.is_lt
                                            ).then_inc(tern_neg_made, 1)
                    dve.wait_ge(tern_neg_made, j + 1)
                    nc.vector.scalar_tensor_tensor(w_tern[j][:], w_ffn[j][:], half_pos[:, j:j + 1], tern_neg[:],
                                                   ALU.is_gt, ALU.subtract).then_inc(tern_made, 1)
                elif name.startswith("ln_stats"):
                    layernorm_stats(int(name[-1]) - 1, b)
                elif name.startswith("ln_apply"):
                    k = int(name[-1]) - 1
                    layernorm_apply(k, b, xn_before.get((k, b)))
                    if k == 0 and b == 0:
                        dve.wait_ge(w_hi_made, 1)
                        nc.vector.tensor_tensor(w_qkv_lo[:], w_qkv[:], w_qkv_hi[:].bitcast(F32), ALU.subtract
                                                ).then_inc(w_lo_made, 1)
                elif name == "ln_turn1":
                    dve.wait_ge(lnT_hi[0], b + 1)
                    nc.vector.tensor_tensor(xT_lo[:], misc_bank[:].rearrange("p (k t) -> p k t", k=CT),
                                            xT_hi[:].bitcast(F32), ALU.subtract).then_inc(lnT_lo[0], 1)
                elif name == "ln_turn3":
                    dve.wait_ge(lnT_hi[2], b + 1)
                    nc.vector.tensor_tensor(x3T[:, 1], misc_bank[:].rearrange("p (k t) -> p k t", k=CT),
                                            x3T[:, 0], ALU.subtract).then_inc(lnT_lo[2], 1)
                elif name == "qk":
                    n = 2 * b + j
                    bank = dense_bank[dense_at[(name, b, j)]]
                    dve.wait_ge(qk_projected, n + 1)
                    if b:
                        dve.wait_ge(qk_rotated, n - 1)
                        dve.wait_ge(qk_hi, n - 1)
                        dve.wait_ge(qk_lo, n - 1)
                    nc.vector.stream_shuffle(swapped[j][:].rearrange("p k t -> p (k t)"), bank[:],
                                             [i ^ 1 for i in range(32)]).then_inc(qk_swapped, 1)
                    nc.vector.tensor_tensor(turned[j][:], bank[:].rearrange("p (k t) -> p k t", k=CT),
                                            cos_t.rearrange("p (k t) -> p k t", k=1).broadcast_to((P, CT, T)),
                                            ALU.mult).then_inc(qk_cos, 1)
                elif name == "pack":
                    n = 2 * b + j
                    dve.wait_ge(qk_hi, n + 1)
                    if b:
                        dve.wait_ge(scratch_written[j], 16 * b)
                    nc.vector.tensor_tensor(parts[j][:, 1], turned[j][:], parts[j][:, 0].bitcast(F32), ALU.subtract
                                            ).then_inc(qk_lo, 1)
                elif name == "sq":
                    n = SQ_STEPS * b + j
                    dve.wait_ge(sq_made, n + 1)
                    if j == 0 and b:
                        dve.wait_ge(max_lo, b)
                    if j < 4:
                        into, heads = neg_max[:, 0, 4 * j:4 * j + 4], 4
                    else:
                        into, heads = neg_max[:, 1, 2 * (j - 4):2 * (j - 4) + 2], 2
                    nc.vector.tensor_reduce(into, sq_bank[n % 2][:].rearrange("p (h k) -> p h k", h=heads), AX.X,
                                            ALU.max, negate=True).then_inc(sq_maxed, 1)
                elif name == "max_rows":
                    dve.wait_ge(sq_maxed, SQ_STEPS * (b + 1))
                    if b:
                        dve.wait_ge(max_turned, b)
                    nc.vector.tensor_copy(max_parts[:, :, 0], neg_max[:]).then_inc(max_hi, 1)
                    dve.wait_ge(max_hi, b + 1)
                    nc.vector.tensor_tensor(max_parts[:, :, 1], neg_max[:], max_parts[:, :, 0].bitcast(F32),
                                            ALU.subtract).then_inc(max_lo, 1)
                elif name == "y_turn":
                    n = TT * b + j
                    dve.wait_ge(y_turned, n + 1)
                    if b:
                        dve.wait_ge(yn_turned, b)
                    bank = misc_bank[:].rearrange("p (h d) -> p h d", d=32)
                    nc.vector.reciprocal(y_rec[:, j].rearrange("p (h a) -> p h a", a=1), bank[:, :, D:D + 1]
                                         ).then_inc(y_rec_made, 1)
                    dve.wait_ge(y_rec_made, n + 1)
                    nc.vector.tensor_tensor(yn[:, j].rearrange("p (h d) -> p h d", d=D), bank[:, :, 0:D],
                                            y_rec[:, j].rearrange("p (h a) -> p h a", a=1).broadcast_to((P, H, D)),
                                            ALU.mult).then_inc(y_normed, 1)
                elif name == "proj":
                    dve.wait_ge(projected, b + 1)
                    nc.vector.tensor_tensor(x[:, b], misc_bank[:].rearrange("p (i c) -> p i c", i=TT), x[:, b], ALU.add
                                            ).then_inc(x1_made, 1)
                elif name == "cross":
                    dve.wait_ge(crossed, b + 1)
                    nc.vector.tensor_tensor(x[:, b], misc_bank[:].rearrange("p (i c) -> p i c", i=TT), x[:, b], ALU.add
                                            ).then_inc(x2_made, 1)
                elif name == "ctx_scores":
                    dve.wait_ge(ctx_scored, b + 1)
                    if b:
                        dve.wait_ge(ctx_exped, TT * b)
                    nc.vector.tensor_reduce(ctx_negmax[:], misc_bank[:].rearrange("p (i n) -> p i n", i=TT), AX.X,
                                            ALU.max, negate=True).then_inc(ctx_maxed, 1)
                elif name == "ctx_turn":
                    dve.wait_ge(ctx_exped, TT * (b + 1))
                    if b:
                        dve.wait_ge(ctx_turned, b)
                    nc.vector.reciprocal(ctx_rec[:], ctx_sum[:]).then_inc(ctx_rec_made, 1)
                    dve.wait_ge(ctx_rec_made, b + 1)
                    for i in range(TT):
                        nc.vector.tensor_scalar(ctx_attn[:, i], ctx_exp[:, i], ctx_rec[:, i:i + 1], None, ALU.mult
                                                ).then_inc(ctx_normed, 1)
                elif name == "up_gate":
                    n = ET * b + j
                    bank = dense_bank[dense_at[(name, b, j)]]
                    dve.wait_ge(tanh_made, n + 1)
                    if n >= 2:
                        dve.wait_ge(hid_hi, n - 1)
                        dve.wait_ge(hid_lo, n - 1)
                    nc.vector.scalar_tensor_tensor(act_up[n % 2], tanh_up[n % 2], 1.0, bank[:, 0:T], ALU.add,
                                                   ALU.mult).then_inc(act_made, 1)
                    dve.wait_ge(act_made, n + 1)
                    nc.vector.scalar_tensor_tensor(hidden[n % 2], bank[:, T:2 * T], 0.125, act_up[n % 2],
                                                   ALU.mult, ALU.mult).then_inc(hidden_made, 1)
                elif name == "down":
                    dve.wait_ge(down_made, b + 1)
                    dve.wait_ge(out_scale_made, 2)
                    if b:
                        dve.wait_ge(stored, 16 * b)
                    nc.vector.scalar_tensor_tensor(
                        result.rearrange("p i c -> p (i c)"), dense_bank[dense_at[(name, b, j)]][:],
                        out_scale[:, 1:2], x[:, b].rearrange("p i c -> p (i c)"), ALU.mult, ALU.add
                    ).then_inc(result_made, 1)

        @block.tensor
        def _(pe):
            def turn(dst, src, signal):
                for i in range(TT):
                    for k in range(CT):
                        last = nc.tensor.transpose(dst[:, k * T + i * P:k * T + (i + 1) * P],
                                                   src[:, i, k * P:(k + 1) * P], ident)
                last.then_inc(signal, 1)

            for step in ORDER:
                name, b, j = step
                if name == "ternary" and j == 0:
                    free_misc(pe, step)
                    pe.wait_ge(ones_set, 1)
                    pe.wait_ge(abs_summed, 3)
                    nc.tensor.matmul(misc_bank[:, 0:3], ones[:], abs_sum[:], start=True, stop=True
                                     ).then_inc(abs_total, 1)
                elif name.startswith("ln_turn"):
                    k = int(name[-1]) - 1
                    pe.wait_ge(normed[k], TT * (b + 1))
                    pe.wait_ge(consts_loaded, 16)
                    free_misc(pe, step)
                    turn(misc_bank, xn, turned_ln[k])
                elif name == "qk":
                    pe.wait_ge(lnT_lo[0], b + 1)
                    pe.wait_ge(w_lo_made, 1)
                    free_dense(pe, step)
                    bank = dense_bank[dense_at[step]]
                    for m in range(CT):
                        terms = [(k, w, a) for k in range(CT) for w, a in
                                 ((w_qkv_hi, xT_hi), (w_qkv_hi, xT_lo), (w_qkv_lo, xT_hi))]
                        for t, (k, w, a) in enumerate(terms):
                            last = nc.tensor.matmul(bank[:, m * T:(m + 1) * T],
                                                    w[:, k, j * C + m * P:j * C + (m + 1) * P], a[:, k, :],
                                                    start=(t == 0), stop=(t == len(terms) - 1))
                    last.then_inc(qk_projected, 1)
                elif name == "v":
                    free_misc(pe, step)
                    for i in range(TT):
                        terms = [(k, w, a) for k in range(CT) for w, a in
                                 ((w_qkv_hi, xT_hi), (w_qkv_hi, xT_lo), (w_qkv_lo, xT_hi))]
                        for t, (k, w, a) in enumerate(terms):
                            last = nc.tensor.matmul(misc_bank[:, i * C:(i + 1) * C], a[:, k, i * P:(i + 1) * P],
                                                    w[:, k, 2 * C:3 * C], start=(t == 0), stop=(t == len(terms) - 1))
                    last.then_inc(v_projected, 1)
                elif name == "sq":
                    n = SQ_STEPS * b + j
                    bank = sq_bank[n % 2]
                    q, k = pack[0][b % 2], pack[1][b % 2]
                    if j == 0:
                        pe.wait_ge(ident16_made, 1)
                        pe.wait_ge(mask_made, 1)
                        pe.wait_ge(pack_rows_set, 3)
                        pe.wait_ge(key_rows_set, 1)
                        for s in range(2):
                            pe.wait_ge(packed[s][b % 2], 16 * TERMS * (b // 2 + 1))
                    if n >= 2:
                        pe.wait_ge(sq_maxed, n - 1)
                    if j < 4:
                        nc.tensor.matmul(bank[:], ident16[:], mask16[:].rearrange("p a k -> p (a k)"), start=True,
                                         stop=False, skip_group_check=True)
                        for a in range(4):
                            h = 4 * j + a
                            last = nc.tensor.matmul(bank[:, a * P:(a + 1) * P], q[0:MROW, h, 0:P], k[0:MROW, h, 0:P],
                                                    start=False, stop=(a == 3), skip_group_check=True)
                    else:
                        nc.tensor.matmul(bank[:].rearrange("p (h k) -> p h k", h=2)[:, :, P:T], ident16[:],
                                         mask16[:, 0:2, :], start=True, stop=False, skip_group_check=True)
                        for a in range(2):
                            h = 2 * (j - 4) + a
                            last = nc.tensor.matmul(bank[:, a * T:(a + 1) * T], q[0:MROW, h, P:T], k[0:MROW, h, :],
                                                    start=False, stop=(a == 1), skip_group_check=True)
                    last.then_inc(sq_made, 1)
                elif name == "max_rows":
                    pe.wait_ge(max_lo, b + 1)
                    free_misc(pe, step)
                    for i in range(TT):
                        last = nc.tensor.transpose(misc_bank[0:32, i * P:(i + 1) * P],
                                                   max_parts[:, i].rearrange("p a h -> p (a h)").bitcast(F32), ident)
                    last.then_inc(max_turned, 1)
                elif name == "st":
                    n = ST_STEPS * b + j
                    bank = st_bank[n % 2]
                    q, k = pack[0][b % 2], pack[1][b % 2]
                    if j == 0:
                        pe.wait_ge(max_placed[b % 2], 32 * (b // 2 + 1))
                    if n >= 2:
                        pe.wait_ge(exp_made, n - 1)
                    g, u = j // 3, j % 3
                    K = MROW + ONES_ROW
                    if u < 2:
                        for a in range(2):
                            h = 4 * g + 2 * u + a
                            last = nc.tensor.matmul(bank[:, a * T:(a + 1) * T], k[0:K, h, 0:P], q[0:K, h, :],
                                                    start=True, stop=True)
                    else:
                        for a in range(4):
                            h = 4 * g + a
                            last = nc.tensor.matmul(bank[:, a * P:(a + 1) * P], k[0:K, h, P:T], q[0:K, h, P:T],
                                                    start=True, stop=True)
                    last.then_inc(st_made, 1)
                elif name == "pv":
                    n = G * b + j
                    pe.wait_ge(probs_masked, 2 * (n + 1))
                    if j == 0:
                        pe.wait_ge(v_stored, b + 1)
                    if n % 2 == 0 and n:
                        pe.wait_ge(y_stored, n // 2)
                    pr, va, off = probs[n % 2], v_aug[b % 2], (j % 2) * T
                    for a in range(4):
                        nc.tensor.matmul(pv_bank[32 * a:32 * a + 32, off:off + T], va[:, 0, 4 * j + a, :],
                                         pr[:, a // 2, (a % 2) * T:(a % 2) * T + T], start=True, stop=False,
                                         skip_group_check=True)
                    for a in range(4):
                        last = nc.tensor.matmul(pv_bank[32 * a:32 * a + 32, off + P:off + T], va[:, 1, 4 * j + a, :],
                                                pr[:, 2, a * P:(a + 1) * P], start=False, stop=True,
                                                skip_group_check=True)
                    last.then_inc(pv_made, 1)
                elif name == "y_turn":
                    pe.wait_ge(y_stored, 2 * (b + 1))
                    free_misc(pe, step)
                    for g in range(G):
                        last = nc.tensor.transpose(misc_bank[:, g * P:(g + 1) * P], yT_raw[:, g, j * P:(j + 1) * P],
                                                   ident)
                    last.then_inc(y_turned, 1)
                elif name == "yn_turn":
                    pe.wait_ge(y_normed, TT * (b + 1))
                    free_misc(pe, step)
                    turn(misc_bank, yn, yn_turned)
                elif name == "proj":
                    pe.wait_ge(ynT_stored, b + 1)
                    pe.wait_ge(wproj_loaded, 16)
                    free_misc(pe, step)
                    for i in range(TT):
                        for k in range(CT):
                            last = nc.tensor.matmul(misc_bank[:, i * C:(i + 1) * C], ynT[:, k, i * P:(i + 1) * P],
                                                    w_proj[:, k, :], start=(k == 0), stop=(k == CT - 1))
                    last.then_inc(projected, 1)
                elif name == "cross":
                    pe.wait_ge(lnT_hi[1], b + 1)
                    pe.wait_ge(attnT_stored, b + 1)
                    free_misc(pe, step)
                    for i in range(TT):
                        for k in range(CT):
                            last = nc.tensor.matmul(misc_bank[:, i * C:(i + 1) * C], x2T[:, k, i * P:(i + 1) * P],
                                                    attnT[b % 2][:, k, :], start=(k == 0), stop=(k == CT - 1))
                    last.then_inc(crossed, 1)
                elif name == "ctx_qk":
                    pe.wait_ge(ctx_loaded, 48)
                    free_misc(pe, step)
                    for a in range(2):
                        last = nc.tensor.matmul(misc_bank[:, a * T:(a + 1) * T], w_ctx[:, a, :], ctxT[:, b, :],
                                                start=True, stop=True)
                    last.then_inc(ctx_projected, 1)
                elif name == "ctx_scores":
                    pe.wait_ge(ctx_qk_made, 2 * (b + 1))
                    free_misc(pe, step)
                    for i in range(TT):
                        last = nc.tensor.matmul(misc_bank[:, i * T:(i + 1) * T], ctx_qk[:, 0, i * P:(i + 1) * P],
                                                ctx_qk[:, 1, :], start=True, stop=True)
                    last.then_inc(ctx_scored, 1)
                elif name == "ctx_turn":
                    pe.wait_ge(ctx_normed, TT * (b + 1))
                    free_misc(pe, step)
                    turn(misc_bank, ctx_attn, ctx_turned)
                elif name == "up_gate":
                    if j == 0:
                        pe.wait_ge(lnT_lo[2], b + 1)
                        pe.wait_ge(tern_made, 2)
                    free_dense(pe, step)
                    bank = dense_bank[dense_at[step]]
                    for w in range(2):
                        wt = w_tern[w][:].rearrange("p (k n) -> p k n", k=CT)
                        for t in range(2 * CT):
                            last = nc.tensor.matmul(bank[:, w * T:(w + 1) * T], wt[:, t // 2, j * P:(j + 1) * P],
                                                    x3T[:, t % 2, t // 2, :], start=(t == 0), stop=(t == 2 * CT - 1))
                    last.then_inc(up_gate_made, 1)
                elif name == "down":
                    pe.wait_ge(hid_lo, ET * (b + 1))
                    pe.wait_ge(tern_made, 3)
                    free_dense(pe, step)
                    bank = dense_bank[dense_at[step]]
                    wt = w_tern[2][:].rearrange("p (k n) -> p k n", k=ET)
                    for i in range(TT):
                        for t in range(2 * ET):
                            last = nc.tensor.matmul(bank[:, i * C:(i + 1) * C], hid[:, t % 2, t // 2, i * P:(i + 1) * P],
                                                    wt[:, t // 2, :], start=(t == 0), stop=(t == 2 * ET - 1))
                    last.then_inc(down_made, 1)


def constants():
    theta = (1.0 / 10000.0 ** (np.arange(0, D, 2, dtype=np.float32) / np.float32(D))).astype(np.float32)
    angle = np.outer(np.arange(T, dtype=np.float32), theta).astype(np.float32)
    channel = np.arange(P) % D
    cos = np.cos(angle).astype(np.float32)[:, channel // 2].T
    sin = np.sin(angle).astype(np.float32)[:, channel // 2].T
    sin = sin * np.where(channel % 2 == 0, -1.0, 1.0).astype(np.float32)[:, None]
    return np.ascontiguousarray(np.concatenate([np.eye(P, dtype=np.float32), cos, sin], axis=1))


def kernel(**inputs):
    import concourse.bacc as bacc
    from concourse.bass_utils import run_bass_kernel_spmd

    a = {k: np.asarray(v) for k, v in inputs.items()}
    arrays = {
        "x": a["x"],
        "ctxT": a["ctx_1024"].transpose(0, 2, 1),
        "wqkvT": a["L0_attn_w_atten"].T,
        "wpT": a["L0_attn_w_proj"].T,
        "wctxT": np.stack([a["L0_xattn_Wq"].T, a["L0_xattn_Wk"].T]),
        "bctx": np.stack([a["L0_xattn_bq"], a["L0_xattn_bk"]], axis=1),
        "wupT": a["L0_ffn_W_up"].T,
        "wgateT": a["L0_ffn_W_gate"].T,
        "wdownT": a["L0_ffn_W_down"].T,
        "consts": constants(),
    }
    arrays = {f"in_{k}": np.ascontiguousarray(v) for k, v in arrays.items()}
    nc = bacc.Bacc("TRN2", target_bir_lowering=False, num_devices=1)
    args = [nc.dram_tensor(k, v.shape, mybir.dt.from_np(v.dtype), kind="ExternalInput").ap() for k, v in arrays.items()]
    out = nc.dram_tensor("out", (B, T, C), F32, kind="ExternalOutput").ap()
    decoder_kernel(nc, *args, out)
    r = run_bass_kernel_spmd(nc, [arrays], core_ids=[0])
    return r.results[0]["out"]
```

```python
from contextlib import ExitStack

import numpy as np

import concourse.bass as bass
from concourse import mybir

F32 = mybir.dt.float32
F32R = mybir.dt.float32r
F16 = mybir.dt.float16
BF16 = mybir.dt.bfloat16
ALU = mybir.AluOpType
ACT = mybir.ActivationFunctionType
AX = mybir.AxisListType

P = 128
B = 4
T = 256
C = 256
H = 16
D = C // H
E = 1024
DX = 128
TT = T // P
CT = C // P
ET = E // P
G = H // 4
TERMS = 4
ROWS = TERMS * D
MROW = 96
ONES_ROW = 2
EPS_LN = 1e-5
EPS_Q = 1e-8
MASKED = -1e30
SQ_STEPS = TT * 2 + H // 2
ST_STEPS = 3 * G


PE, DVE, ACTE, POOL, SP = "tensor", "vector", "scalar", "gpsimd", "sync"
SEMAPHORE_NS = 220
COUNT = {"qk": 2, "rotate": 2, "rotate_add": 2, "qk_hi": 2, "qk_lo": 2, "scratch": 2, "pack": 2,
         "sq": SQ_STEPS, "sq_max": SQ_STEPS, "st": ST_STEPS, "exp": ST_STEPS, "mask": G, "pv": G, "y_store": 2,
         "y_turn": TT, "y_norm": TT, "up_gate": ET, "tanh": ET, "act": ET, "hidden": ET, "hid_hi": ET, "hid_lo": ET}
PARTS = {
    "ctx_qk": (PE, 860), "ctx_bias": (ACTE, 700), "ctx_scores": (PE, 860), "ctx_max": (DVE, 600),
    "ctx_exp": (ACTE, 900), "ctx_norm": (DVE, 700), "ctx_turn": (PE, 430), "ctx_store": (ACTE, 480),
    "stats1": (DVE, 1250), "stats2": (DVE, 1250), "stats3": (DVE, 1250),
    "rstd1": (POOL, 630), "rstd2": (POOL, 630), "rstd3": (POOL, 630),
    "apply1": (DVE, 420), "apply2": (DVE, 420), "apply3": (DVE, 420),
    "ln_turn1": (PE, 430), "ln_turn2": (PE, 430), "ln_turn3": (PE, 430),
    "ln_hi1": (ACTE, 480), "ln_hi2": (ACTE, 480), "ln_hi3": (ACTE, 480), "ln_lo1": (DVE, 600), "ln_lo3": (DVE, 600),
    "qk": (PE, 1310), "rotate": (DVE, 1200), "rotate_add": (POOL, 2500), "qk_hi": (ACTE, 520), "qk_lo": (DVE, 600),
    "scratch": (SP, 600), "pack": (SP, 2400), "v": (PE, 1310), "v_store": (ACTE, 480),
    "sq": (PE, 380), "sq_max": (DVE, 600), "max_split": (DVE, 350), "max_turn": (PE, 200), "max_store": (ACTE, 270),
    "max_rows": (SP, 1200), "st": (PE, 230), "exp": (ACTE, 480), "mask": (POOL, 1200), "pv": (PE, 780),
    "y_store": (ACTE, 480), "y_turn": (PE, 430), "y_norm": (DVE, 650), "yn_turn": (PE, 430), "yn_store": (ACTE, 480),
    "proj": (PE, 1720), "add1": (DVE, 600), "cross": (PE, 1720), "add2": (DVE, 600),
    "up_gate": (PE, 870), "tanh": (ACTE, 360), "act": (DVE, 340), "hidden": (DVE, 340), "hid_hi": (ACTE, 310),
    "hid_lo": (POOL, 630), "down": (PE, 3500), "result": (DVE, 660), "store": (SP, 600),
    "w_hi": (ACTE, 1400), "w_lo": (DVE, 1700), "abs": (ACTE, 1900), "abs_total": (PE, 500), "scales": (DVE, 700),
    "ternary": (DVE, 3600),
}
ONCE = {"w_hi": 1, "w_lo": 1, "abs": 3, "abs_total": 1, "scales": 1, "ternary": 3}
EXTRA_NS = {"scratch": 2200, "pack": 3500, "max_rows": 2200}
FREED_BY = {"ctx_qk": "ctx_bias", "ctx_scores": "ctx_exp", "ctx_turn": "ctx_store", "ln_turn1": "ln_lo1",
            "ln_turn2": "ln_hi2", "ln_turn3": "ln_lo3", "qk": "rotate", "v": "v_store", "sq": "sq_max",
            "max_turn": "max_store", "st": "exp", "y_turn": "y_norm", "yn_turn": "yn_store", "proj": "add1",
            "cross": "add2", "up_gate": "hidden", "down": "result", "abs_total": "scales", "pv": "y_store"}


def needs(name, b, j):
    def n(other, k, count=1):
        return (other, k // count, k % count)

    table = {
        "ctx_bias": [("ctx_qk", b, 0), ("ctx_scores", b - 1, 0)],
        "ctx_scores": [("ctx_bias", b, 0)],
        "ctx_max": [("ctx_scores", b, 0), ("ctx_exp", b - 1, 0)],
        "ctx_exp": [("ctx_max", b, 0), ("ctx_norm", b - 1, 0)],
        "ctx_norm": [("ctx_exp", b, 0), ("ctx_turn", b - 1, 0)],
        "ctx_turn": [("ctx_norm", b, 0)],
        "ctx_store": [("ctx_turn", b, 0), ("cross", b - 2, 0)],
        "stats1": [("apply1", b - 1, 0)],
        "stats2": [("add1", b, 0), ("apply2", b - 1, 0)],
        "stats3": [("add2", b, 0), ("apply3", b - 1, 0)],
        "ln_hi1": [("ln_turn1", b, 0), ("v", b - 1, 0), ("qk", b - 1, 1), ("ln_lo1", b - 1, 0)],
        "ln_hi2": [("ln_turn2", b, 0), ("cross", b - 1, 0)],
        "ln_hi3": [("ln_turn3", b, 0), ("up_gate", b - 1, ET - 1), ("ln_lo3", b - 1, 0), ("ternary", 0, 2)],
        "ln_lo1": [("ln_hi1", b, 0)],
        "ln_lo3": [("ln_hi3", b, 0)],
        "w_lo": [("w_hi", 0, 0)],
        "qk": [("ln_lo1", b, 0), ("w_lo", 0, 0)],
        "rotate": [("qk", b, j), ("rotate_add", b - 1, j), ("qk_hi", b - 1, j), ("qk_lo", b - 1, j)],
        "rotate_add": [("rotate", b, j)],
        "qk_hi": [("rotate_add", b, j), ("scratch", b - 1, j)],
        "qk_lo": [("qk_hi", b, j)],
        "scratch": [("qk_lo", b, j)],
        "pack": [("scratch", b, j), ("st", b - 2, ST_STEPS - 1)],
        "v": [("ln_lo1", b, 0), ("w_lo", 0, 0)],
        "v_store": [("v", b, 0), ("pv", b - 2, G - 1)],
        "sq": [("pack", b, 0), ("pack", b, 1)],
        "sq_max": [("sq", b, j), ("max_split", b - 1, 0)],
        "max_split": [("sq_max", b, SQ_STEPS - 1), ("max_turn", b - 1, 0)],
        "max_turn": [("max_split", b, 0)],
        "max_store": [("max_turn", b, 0), ("max_rows", b - 1, 0)],
        "max_rows": [("max_store", b, 0)],
        "st": [("max_rows", b, 0)],
        "exp": [("st", b, j), n("pv", G * b + j // 3 - 2, G)],
        "mask": [("exp", b, 3 * j + 2)],
        "pv": [("mask", b, j), ("v_store", b, 0)],
        "y_store": [("pv", b, 2 * j + 1), ("y_turn", b - 1, TT - 1), ("w_lo", 0, 0)],
        "y_turn": [("y_store", b, 1)],
        "y_norm": [("y_turn", b, j), ("yn_turn", b - 1, 0), ("w_lo", 0, 0)],
        "yn_turn": [("y_norm", b, TT - 1)],
        "yn_store": [("yn_turn", b, 0), ("proj", b - 1, 0)],
        "proj": [("yn_store", b, 0)],
        "add1": [("proj", b, 0)],
        "cross": [("ln_hi2", b, 0), ("ctx_store", b, 0)],
        "add2": [("cross", b, 0)],
        "abs": [("w_hi", 0, 0)],
        "abs_total": [("abs", 0, 2)],
        "scales": [("abs_total", 0, 0)],
        "ternary": [("scales", 0, 0)],
        "up_gate": [("ln_lo3", b, 0), ("ternary", 0, 1)],
        "tanh": [("up_gate", b, j), n("act", ET * b + j - 2, ET)],
        "act": [("tanh", b, j)],
        "hidden": [("act", b, j), n("hid_lo", ET * b + j - 2, ET)],
        "hid_hi": [("hidden", b, j), ("down", b - 1, 0)],
        "hid_lo": [("hid_hi", b, j)],
        "down": [("hid_lo", b, ET - 1), ("ternary", 0, 2)],
        "result": [("down", b, 0), ("store", b - 1, 0)],
        "store": [("result", b, 0)],
    }
    for k in "123":
        table["rstd" + k] = [("stats" + k, b, 0)]
        table["apply" + k] = [("rstd" + k, b, 0), ("ln_turn" + k, b - 1, 0)] + [("ternary", 0, 2)] * (k == "3")
        table["ln_turn" + k] = [("apply" + k, b, 0)]
    found = [x for x in table.get(name, []) if x[1] >= 0]
    count = ONCE.get(name) or COUNT.get(name, 1)
    before = b * count + j - 1
    if before >= 0:
        found.append((name, before // count, before % count))
    return found


def plan(batch_ns=26000, urgency=0.2, banks=8):
    every = [(name, b, j) for name in PARTS for b in range(1 if name in ONCE else B)
             for j in range(ONCE.get(name) or COUNT.get(name, 1))]
    alone = {}

    def nominal(part):
        name, b, j = part
        if part not in alone:
            alone[part] = max([nominal(x) + PARTS[x[0]][1] + EXTRA_NS.get(x[0], 0) + SEMAPHORE_NS
                               for x in needs(name, b, j)] + [b * batch_ns])
        return alone[part]

    ends, order, bank_of, before = {}, {e: [] for e in (PE, DVE, ACTE, POOL, SP)}, {}, {}
    engine_free = dict.fromkeys(order, 0)
    bank_free, bank_last, freeing = [0] * banks, [None] * banks, {}
    left = sorted(every, key=nominal)
    while left:
        best = None
        for part in left:
            name, b, j = part
            if any(x not in ends for x in needs(name, b, j)):
                continue
            engine = PARTS[name][0]
            start = max([engine_free[engine]] + [ends[x] + SEMAPHORE_NS for x in needs(name, b, j)])
            if name in FREED_BY and not (name == "pv" and j % 2):
                if min(bank_free) == float("inf"):
                    continue
                start = max(start, min(bank_free) + SEMAPHORE_NS)
            score = start + urgency * nominal(part)
            if best is None or score < best[0]:
                best = (score, start, part)
        _, start, part = best
        name, b, j = part
        left.remove(part)
        engine, ns = PARTS[name]
        order[engine].append(part)
        engine_free[engine] = start + ns
        ends[part] = start + ns + EXTRA_NS.get(name, 0)
        if name == "pv" and j % 2:
            bank_of[part] = bank_of["pv", b, j - 1]
        elif name in FREED_BY:
            ready = [i for i in range(banks) if bank_free[i] + SEMAPHORE_NS <= start]
            bank = max(ready, key=lambda i: bank_free[i]) if ready else bank_free.index(min(bank_free))
            bank = min(ready, key=lambda i: bank_free[i]) if ready else bank
            bank_of[part], before[part] = bank, bank_last[bank]
            bank_last[bank], bank_free[bank] = part, float("inf")
            freeing[FREED_BY[name], b, j // 2 if name == "pv" else j] = bank
        if part in freeing:
            bank_free[freeing[part]] = ends[part]
    return order, bank_of, before


def decoder_kernel(nc, x_in, ctxT_in, wqkvT_in, wpT_in, wctxT_in, bctx_in, wupT_in, wgateT_in, wdownT_in,
                   consts_in, out):
    ORDER, BANK, BANK_BEFORE = plan()

    with ExitStack() as ctx:
        def sb(name, shape, dt=F32):
            return ctx.enter_context(nc.sbuf_tensor(name, shape, dt))

        def psum(name, shape):
            return ctx.enter_context(nc.psum_tensor(name, shape, F32))

        def sem(name):
            return ctx.enter_context(nc.semaphore(name))

        banks = [psum(f"bank{i}", [P, 512]) for i in range(8)]

        def bank_of(name, b, j):
            return banks[BANK[name, b, j]]

        x = sb("x", [P, B, TT, C])
        w_qkv = sb("w_qkv", [P, CT, 3 * C])
        w_qkv_hi = sb("w_qkv_hi", [P, CT, 3 * C], F32R)
        w_qkv_lo = sb("w_qkv_lo", [P, CT, 3 * C], F32R)
        w_proj = sb("w_proj", [P, CT, C])
        w_ctx = sb("w_ctx", [P, 2, DX])
        b_ctx = sb("b_ctx", [P, 2])
        w_ffn = [sb(f"w_ffn{k}", [P, 2048]) for k in range(3)]
        w_tern = [sb(f"w_tern{k}", [P, 2048], F16) for k in range(3)]
        tern_neg = sb("tern_neg", [P, 2048], F16)
        abs_sum = sb("abs_sum", [P, 3])
        scales = sb("scales", [P, 3])
        half_pos = sb("half_pos", [P, 3])
        half_neg = sb("half_neg", [P, 3])
        out_scale = sb("out_scale", [P, 2])
        consts = sb("consts", [P, P + 2 * T])
        ident = consts[:, 0:P]
        cos_t, sin_t = consts[:, P:P + T], consts[:, P + T:P + 2 * T]
        ident16 = sb("ident16", [P, P], BF16)
        mask16 = sb("mask16", [P, 4, P], BF16)
        ones = sb("ones", [P, P])
        neg_half = sb("neg_half", [P, TT])

        stats = [sb(f"stats{k}", [P, TT, 6]) for k in (1, 2, 3)]
        mean_var = [sb(f"mean_var{k}", [P, TT, 2]) for k in (1, 2, 3)]
        var_eps = [sb(f"var_eps{k}", [P, TT]) for k in (1, 2, 3)]
        rstd = [sb(f"rstd{k}", [P, TT]) for k in (1, 2, 3)]
        spare_down = w_ffn[2][:].rearrange("p (n t) -> p n t", t=T)
        xn = [sb("xn1", [P, TT, C]), sb("xn2", [P, TT, C]), spare_down[:, 0:2]]
        xT_hi = sb("xT_hi", [P, CT, T], F32R)
        xT_lo = sb("xT_lo", [P, CT, T], F32R)
        x2T = sb("x2T", [P, CT, T])
        x3T = spare_down[:, 2:4].bitcast(F16).rearrange("p n (k t) -> p n k t", k=CT)

        swapped = [sb(f"swapped{s}", [P, CT, T]) for s in range(2)]
        turned = [sb(f"turned{s}", [P, CT, T]) for s in range(2)]
        parts = [sb(f"parts{s}", [P, 2, CT, T], F32R) for s in range(2)]
        pack = [[sb(f"pack{s}{i}", [P, H, T], F32R) for i in range(2)] for s in range(2)]
        v_aug = [sb(f"v_aug{i}", [P, TT, H, 32]) for i in range(2)]
        neg_max = sb("neg_max", [P, TT, H])
        max_parts = sb("max_parts", [P, TT, 2, H], F32R)
        maxT = sb("maxT", [32, T])
        probs = [sb(f"probs{i}", [P, 3, 512]) for i in range(2)]
        spare_qkv = w_qkv[:].rearrange("p k n -> p (k n)").rearrange("p (n t) -> p n t", t=T)
        yT_raw = spare_qkv[:, 0:G]
        y_rec = sb("y_rec", [P, TT, H])
        yn = spare_qkv[:, G:G + TT]
        ynT = sb("ynT", [P, CT, T])

        ctxT = sb("ctxT", [P, B, T])
        ctx_qk = sb("ctx_qk", [P, 2, T])
        ctx_negmax = sb("ctx_negmax", [P, TT])
        ctx_sum = sb("ctx_sum", [P, TT])
        ctx_rec = sb("ctx_rec", [P, TT])
        ctx_exp = sb("ctx_exp", [P, TT, T])
        ctx_attn = sb("ctx_attn", [P, TT, T])
        attnT = [sb(f"attnT{i}", [P, CT, T]) for i in range(2)]

        spare = w_ffn[1][:].rearrange("p (n t) -> p n t", t=T)
        tanh_up = [spare[:, i] for i in range(2)]
        act_up = [spare[:, 2 + i] for i in range(2)]
        hidden = [spare[:, 4 + i] for i in range(2)]
        result = spare[:, 6:8]
        hid = w_ffn[0][:].bitcast(F16).rearrange("p (a m t) -> p a m t", a=2, m=ET)

        scratch = nc.dram_tensor("scratch", (2, B, 2, C, T), F32, kind="Internal").ap()

        x_loaded = [sem(f"x_loaded{b}") for b in range(B)]
        wqkv_loaded = sem("wqkv_loaded")
        consts_loaded = sem("consts_loaded")
        ctx_loaded = sem("ctx_loaded")
        wproj_loaded = sem("wproj_loaded")
        ffn_loaded = [sem(f"ffn_loaded{k}") for k in range(3)]
        ones_set = sem("ones_set")
        neg_half_set = sem("neg_half_set")
        ident16_made = sem("ident16_made")
        mask_filled = sem("mask_filled")
        mask_made = sem("mask_made")
        pack_rows_set = sem("pack_rows_set")
        v_ones_set = sem("v_ones_set")
        key_rows_set = sem("key_rows_set")
        w_hi_made = sem("w_hi_made")
        w_lo_made = sem("w_lo_made")
        abs_summed = sem("abs_summed")
        abs_total = sem("abs_total")
        scales_made = sem("scales_made")
        halves_made = sem("halves_made")
        out_scale_made = sem("out_scale_made")
        tern_neg_made = sem("tern_neg_made")
        tern_made = sem("tern_made")
        stats_made = [sem(f"stats_made{k}") for k in (1, 2, 3)]
        moments_made = [sem(f"moments_made{k}") for k in (1, 2, 3)]
        var_made = [sem(f"var_made{k}") for k in (1, 2, 3)]
        rstd_made = [sem(f"rstd_made{k}") for k in (1, 2, 3)]
        normed = [sem(f"normed{k}") for k in (1, 2, 3)]
        turned_ln = [sem(f"turned_ln{k}") for k in (1, 2, 3)]
        lnT_hi = [sem(f"lnT_hi{k}") for k in (1, 2, 3)]
        lnT_lo = [sem(f"lnT_lo{k}") for k in (1, 2, 3)]
        qk_projected = sem("qk_projected")
        qk_swapped = sem("qk_swapped")
        qk_cos = sem("qk_cos")
        qk_sin = sem("qk_sin")
        qk_rotated = sem("qk_rotated")
        qk_hi = sem("qk_hi")
        qk_lo = sem("qk_lo")
        scratch_written = [sem(f"scratch_written{s}") for s in range(2)]
        packed = [[sem(f"packed{s}{i}") for i in range(2)] for s in range(2)]
        v_projected = sem("v_projected")
        v_stored = sem("v_stored")
        sq_made = sem("sq_made")
        sq_maxed = sem("sq_maxed")
        max_hi = sem("max_hi")
        max_lo = sem("max_lo")
        max_turned = sem("max_turned")
        maxT_made = sem("maxT_made")
        max_placed = [sem(f"max_placed{i}") for i in range(2)]
        st_made = sem("st_made")
        exp_made = sem("exp_made")
        probs_masked = sem("probs_masked")
        pv_made = sem("pv_made")
        y_stored = sem("y_stored")
        y_turned = sem("y_turned")
        y_rec_made = sem("y_rec_made")
        y_normed = sem("y_normed")
        yn_turned = sem("yn_turned")
        ynT_stored = sem("ynT_stored")
        projected = sem("projected")
        x1_made = sem("x1_made")
        ctx_projected = sem("ctx_projected")
        ctx_qk_made = sem("ctx_qk_made")
        ctx_scored = sem("ctx_scored")
        ctx_maxed = sem("ctx_maxed")
        ctx_exped = sem("ctx_exped")
        ctx_rec_made = sem("ctx_rec_made")
        ctx_normed = sem("ctx_normed")
        ctx_turned = sem("ctx_turned")
        attnT_stored = sem("attnT_stored")
        crossed = sem("crossed")
        x2_made = sem("x2_made")
        up_gate_made = sem("up_gate_made")
        tanh_made = sem("tanh_made")
        act_made = sem("act_made")
        hidden_made = sem("hidden_made")
        hid_hi = sem("hid_hi")
        hid_lo = sem("hid_lo")
        down_made = sem("down_made")
        result_made = sem("result_made")
        stored = sem("stored")

        FREED = {
            "abs_total": lambda b, j: (scales_made, 1),
            "ln_turn1": lambda b, j: (lnT_lo[0], b + 1),
            "ln_turn2": lambda b, j: (lnT_hi[1], b + 1),
            "ln_turn3": lambda b, j: (lnT_lo[2], b + 1),
            "qk": lambda b, j: (qk_cos, 2 * b + j + 1),
            "v": lambda b, j: (v_stored, b + 1),
            "sq": lambda b, j: (sq_maxed, SQ_STEPS * b + j + 1),
            "max_turn": lambda b, j: (maxT_made, b + 1),
            "st": lambda b, j: (exp_made, ST_STEPS * b + j + 1),
            "pv": lambda b, j: (y_stored, 2 * b + j // 2 + 1),
            "y_turn": lambda b, j: (y_normed, TT * b + j + 1),
            "yn_turn": lambda b, j: (ynT_stored, b + 1),
            "proj": lambda b, j: (x1_made, b + 1),
            "ctx_qk": lambda b, j: (ctx_qk_made, 2 * (b + 1)),
            "ctx_scores": lambda b, j: (ctx_exped, TT * (b + 1)),
            "ctx_turn": lambda b, j: (attnT_stored, b + 1),
            "cross": lambda b, j: (x2_made, b + 1),
            "up_gate": lambda b, j: (hidden_made, ET * b + j + 1),
            "down": lambda b, j: (result_made, b + 1),
        }

        def free_bank(pe, name, b, j):
            former = BANK_BEFORE[name, b, j]
            if former is not None:
                pe.wait_ge(*FREED[former[0]](former[1], former[2]))
            return bank_of(name, b, j)

        block = ctx.enter_context(nc.Block())

        @block.sync
        def _(sp):
            def load(dst, src, signal):
                sp.dma_start(dst, src).then_inc(signal, 16)

            x_v = x_in.rearrange("b (i p) c -> p b i c", p=P)
            out_v = out.rearrange("b (i p) c -> p b i c", p=P)
            load(x[:, 0], x_v[:, 0], x_loaded[0])
            load(w_qkv[:], wqkvT_in.rearrange("(k p) n -> p k n", p=P), wqkv_loaded)
            load(consts[:], consts_in, consts_loaded)
            load(w_ctx[:], wctxT_in.rearrange("a c d -> c a d"), ctx_loaded)
            load(b_ctx[:], bctx_in, ctx_loaded)
            load(ctxT[:], ctxT_in.rearrange("b c t -> c b t"), ctx_loaded)
            load(w_ffn[0][:].rearrange("p (k n) -> p k n", k=CT), wupT_in.rearrange("(k p) n -> p k n", p=P), ffn_loaded[0])
            load(w_ffn[1][:].rearrange("p (k n) -> p k n", k=CT), wgateT_in.rearrange("(k p) n -> p k n", p=P), ffn_loaded[1])
            load(w_ffn[2][:].rearrange("p (k n) -> p k n", k=ET), wdownT_in.rearrange("(k p) n -> p k n", p=P), ffn_loaded[2])
            load(x[:, 1], x_v[:, 1], x_loaded[1])
            load(w_proj[:], wpT_in.rearrange("(k p) n -> p k n", p=P), wproj_loaded)
            load(x[:, 2], x_v[:, 2], x_loaded[2])
            load(x[:, 3], x_v[:, 3], x_loaded[3])
            sp.wait_ge(pack_rows_set, 3)
            sp.wait_ge(key_rows_set, 1)
            for name, b, j in ORDER[SP]:
                if name == "scratch":
                    sp.wait_ge(qk_hi, 2 * b + j + 1)
                    sp.wait_ge(qk_lo, 2 * b + j + 1)
                    sp.dma_start(scratch[j, b].rearrange("a (k p) t -> p a k t", p=P),
                                 parts[j][:].bitcast(F32)).then_inc(scratch_written[j], 16)
                elif name == "pack":
                    sp.wait_ge(scratch_written[j], 16 * (b + 1))
                    if b >= 2:
                        sp.wait_ge(st_made, ST_STEPS * (b - 1))
                    for t in range(TERMS):
                        part = t // 2 if j == 0 else t % 2
                        sp.dma_start(pack[j][b % 2][D * t:D * (t + 1), :, :].bitcast(F32),
                                     scratch[j, b, part].rearrange("(h d) t -> d h t", d=D)
                                     ).then_inc(packed[j][b % 2], 16)
                elif name == "max_rows":
                    sp.wait_ge(maxT_made, b + 1)
                    if b >= 2:
                        sp.wait_ge(st_made, ST_STEPS * (b - 1))
                    for a in range(2):
                        sp.dma_start(pack[0][b % 2][MROW + a:MROW + a + 1, :, :].bitcast(F32),
                                     maxT[H * a:H * (a + 1), :]).then_inc(max_placed[b % 2], 16)
                elif name == "store":
                    sp.wait_ge(result_made, b + 1)
                    sp.dma_start(out_v[:, b], result).then_inc(stored, 16)
            sp.wait_ge(stored, 16 * B)

        @block.gpsimd
        def _(pool):
            nc.gpsimd.memset(neg_half[:], -0.5).then_inc(neg_half_set, 1)
            nc.gpsimd.memset(mask16[:], MASKED).then_inc(mask_filled, 1)
            pool.wait_ge(mask_filled, 1)
            nc.gpsimd.affine_select(out=mask16[:], in_=mask16[:], compare_op=ALU.is_gt, fill=0.0, base=0,
                                    pattern=[[0, 4], [1, P]], channel_multiplier=-1).then_inc(mask_made, 1)
            pool.wait_ge(mask_made, 1)
            nc.gpsimd.memset(pack[0][0][64:P].bitcast(F32), 0.0).then_inc(pack_rows_set, 1)
            for n, i in enumerate(range(2)):
                pool.wait_ge(pack_rows_set if i == 0 else v_ones_set, 1)
                nc.gpsimd.memset(v_aug[i][:, :, :, D:32], 1.0).then_inc(v_ones_set, 1)
            pool.wait_ge(v_ones_set, 2)
            nc.gpsimd.memset(pack[0][1][64:P].bitcast(F32), 0.0).then_inc(pack_rows_set, 1)
            pool.wait_ge(pack_rows_set, 2)
            nc.gpsimd.memset(pack[1][1][64:P].bitcast(F32), 1.0).then_inc(pack_rows_set, 1)
            pool.wait_ge(pack_rows_set, 3)
            for name, b, j in ORDER[POOL]:
                if name.startswith("rstd"):
                    k = int(name[-1]) - 1
                    pool.wait_ge(var_made[k], b + 1)
                    pool.wait_ge(neg_half_set, 1)
                    nc.gpsimd.tensor_tensor(rstd[k][:], var_eps[k][:], neg_half[:], ALU.pow).then_inc(rstd_made[k], 1)
                elif name == "rotate_add":
                    n = 2 * b + j
                    pool.wait_ge(qk_swapped, n + 1)
                    nc.gpsimd.tensor_tensor(swapped[j][:], swapped[j][:],
                                            sin_t.rearrange("p (k t) -> p k t", k=1).broadcast_to((P, CT, T)),
                                            ALU.mult).then_inc(qk_sin, 1)
                    pool.wait_ge(qk_sin, n + 1)
                    pool.wait_ge(qk_cos, n + 1)
                    nc.gpsimd.tensor_tensor(turned[j][:], turned[j][:], swapped[j][:], ALU.add).then_inc(qk_rotated, 1)
                elif name == "mask":
                    n = G * b + j
                    pr = probs[n % 2]
                    pool.wait_ge(exp_made, 3 * (n + 1))
                    for sel in (pr[:, 0:2, :].rearrange("p u (h q) -> p (u h) q", q=T)[:, :, 0:P],
                                pr[:, 2, :].rearrange("p (h q) -> p h q", q=P)):
                        nc.gpsimd.affine_select(out=sel, in_=sel, compare_op=ALU.is_ge, fill=0.0, base=0,
                                                pattern=[[0, 4], [1, P]], channel_multiplier=-1
                                                ).then_inc(probs_masked, 1)
                elif name == "hid_lo":
                    n = ET * b + j
                    pool.wait_ge(hid_hi, n + 1)
                    nc.gpsimd.tensor_tensor(hid[:, 1, j], hidden[n % 2], hid[:, 0, j], ALU.subtract
                                            ).then_inc(hid_lo, 1)

        @block.scalar
        def _(act):
            for name, b, j in ORDER[ACTE]:
                if name == "w_hi":
                    act.wait_ge(wqkv_loaded, 16)
                    nc.scalar.activation(w_qkv_hi[:], w_qkv[:], ACT.Copy).then_inc(w_hi_made, 1)
                elif name == "abs":
                    act.wait_ge(ffn_loaded[j], 16)
                    if j:
                        act.wait_ge(abs_summed, j)
                    nc.scalar.activation(tern_neg[:], w_ffn[j][:], ACT.Abs, accum_out=abs_sum[:, j:j + 1]
                                         ).then_inc(abs_summed, 1)
                elif name == "ln_hi1":
                    act.wait_ge(turned_ln[0], b + 1)
                    if b:
                        act.wait_ge(v_projected, b)
                        act.wait_ge(qk_projected, 2 * b)
                        act.wait_ge(lnT_lo[0], b)
                    nc.scalar.activation(xT_hi[:], bank_of("ln_turn1", b, 0)[:].rearrange("p (k t) -> p k t", k=CT),
                                         ACT.Copy).then_inc(lnT_hi[0], 1)
                elif name == "ln_hi2":
                    act.wait_ge(turned_ln[1], b + 1)
                    if b:
                        act.wait_ge(crossed, b)
                    nc.scalar.activation(x2T[:], bank_of("ln_turn2", b, 0)[:].rearrange("p (k t) -> p k t", k=CT),
                                         ACT.Copy).then_inc(lnT_hi[1], 1)
                elif name == "ln_hi3":
                    act.wait_ge(turned_ln[2], b + 1)
                    act.wait_ge(tern_made, 3)
                    if b:
                        act.wait_ge(up_gate_made, ET * b)
                        act.wait_ge(lnT_lo[2], b)
                    nc.scalar.activation(x3T[:, 0], bank_of("ln_turn3", b, 0)[:].rearrange("p (k t) -> p k t", k=CT),
                                         ACT.Copy).then_inc(lnT_hi[2], 1)
                elif name == "qk_hi":
                    act.wait_ge(qk_rotated, 2 * b + j + 1)
                    if b:
                        act.wait_ge(scratch_written[j], 16 * b)
                    nc.scalar.activation(parts[j][:, 0], turned[j][:], ACT.Copy).then_inc(qk_hi, 1)
                elif name == "v_store":
                    act.wait_ge(v_projected, b + 1)
                    act.wait_ge(v_ones_set, 2)
                    if b >= 2:
                        act.wait_ge(pv_made, G * (b - 1))
                    nc.scalar.activation(v_aug[b % 2][:, :, :, 0:D],
                                         bank_of("v", b, 0)[:].rearrange("p (k h d) -> p k h d", k=TT, h=H), ACT.Copy
                                         ).then_inc(v_stored, 1)
                elif name == "max_store":
                    act.wait_ge(max_turned, b + 1)
                    if b:
                        act.wait_ge(max_placed[(b - 1) % 2], 32 * ((b - 1) // 2 + 1))
                    nc.scalar.activation(maxT[:], bank_of("max_turn", b, 0)[0:32, 0:T], ACT.Copy
                                         ).then_inc(maxT_made, 1)
                elif name == "exp":
                    n = ST_STEPS * b + j
                    g = n // 3
                    act.wait_ge(st_made, n + 1)
                    if g >= 2:
                        act.wait_ge(pv_made, g - 1)
                    nc.scalar.activation(probs[g % 2][:, j % 3, :], bank_of("st", b, j)[:], ACT.Exp, scale=D ** -0.5
                                         ).then_inc(exp_made, 1)
                elif name == "y_store":
                    act.wait_ge(pv_made, G * b + 2 * j + 2)
                    act.wait_ge(w_lo_made, 1)
                    if b:
                        act.wait_ge(y_turned, TT * b)
                    nc.scalar.activation(yT_raw[:, 2 * j:2 * j + 2, :],
                                         bank_of("pv", b, 2 * j)[:].rearrange("p (g t) -> p g t", g=2), ACT.Copy
                                         ).then_inc(y_stored, 1)
                elif name == "yn_store":
                    act.wait_ge(yn_turned, b + 1)
                    if b:
                        act.wait_ge(projected, b)
                    nc.scalar.activation(ynT[:], bank_of("yn_turn", b, 0)[:].rearrange("p (k t) -> p k t", k=CT),
                                         ACT.Copy).then_inc(ynT_stored, 1)
                elif name == "ctx_bias":
                    act.wait_ge(ctx_projected, b + 1)
                    act.wait_ge(ctx_loaded, 48)
                    if b:
                        act.wait_ge(ctx_scored, b)
                    for a in range(2):
                        nc.scalar.activation(ctx_qk[:, a], bank_of("ctx_qk", b, 0)[:, a * T:(a + 1) * T],
                                             ACT.Identity, bias=b_ctx[:, a:a + 1]).then_inc(ctx_qk_made, 1)
                elif name == "ctx_exp":
                    act.wait_ge(ctx_maxed, b + 1)
                    if b:
                        act.wait_ge(ctx_normed, TT * b)
                    for i in range(TT):
                        nc.scalar.activation(ctx_exp[:, i], bank_of("ctx_scores", b, 0)[:, i * T:(i + 1) * T],
                                             ACT.Exp, bias=ctx_negmax[:, i:i + 1], accum_out=ctx_sum[:, i:i + 1]
                                             ).then_inc(ctx_exped, 1)
                elif name == "ctx_store":
                    act.wait_ge(ctx_turned, b + 1)
                    if b >= 2:
                        act.wait_ge(crossed, b - 1)
                    nc.scalar.activation(attnT[b % 2][:], bank_of("ctx_turn", b, 0)[:].rearrange(
                        "p (k t) -> p k t", k=CT), ACT.Copy).then_inc(attnT_stored, 1)
                elif name == "tanh":
                    n = ET * b + j
                    act.wait_ge(up_gate_made, n + 1)
                    act.wait_ge(halves_made, 2)
                    if n >= 2:
                        act.wait_ge(act_made, n - 1)
                    nc.scalar.activation(tanh_up[n % 2], bank_of("up_gate", b, j)[:, 0:T], ACT.Tanh,
                                         scale=half_pos[:, 0:1]).then_inc(tanh_made, 1)
                elif name == "hid_hi":
                    n = ET * b + j
                    act.wait_ge(hidden_made, n + 1)
                    if b and j == 0:
                        act.wait_ge(down_made, b)
                    nc.scalar.activation(hid[:, 0, j], hidden[n % 2], ACT.Copy).then_inc(hid_hi, 1)

        @block.vector
        def _(dve):
            nc.vector.memset(ones[:], 1.0).then_inc(ones_set, 1)
            nc.vector.memset(pack[1][0][64:P].bitcast(F32), 1.0).then_inc(key_rows_set, 1)

            dve.wait_ge(consts_loaded, 16)
            nc.vector.tensor_copy(ident16[:], ident).then_inc(ident16_made, 1)
            for name, b, j in ORDER[DVE]:
                if name == "scales":
                    dve.wait_ge(abs_total, 1)
                    nc.vector.tensor_scalar(scales[:], bank_of("abs_total", 0, 0)[:, 0:3], 1.0 / (C * E), EPS_Q,
                                            ALU.mult, ALU.add).then_inc(scales_made, 1)
                    dve.wait_ge(scales_made, 1)
                    nc.vector.tensor_scalar(half_pos[:], scales[:], 0.5, None, ALU.mult).then_inc(halves_made, 1)
                    nc.vector.tensor_scalar(half_neg[:], scales[:], -0.5, None, ALU.mult).then_inc(halves_made, 1)
                    nc.vector.tensor_tensor(out_scale[:, 0:1], scales[:, 0:1], scales[:, 1:2], ALU.mult
                                            ).then_inc(out_scale_made, 1)
                    dve.wait_ge(out_scale_made, 1)
                    nc.vector.tensor_scalar(out_scale[:, 1:2], out_scale[:, 0:1], scales[:, 2:3], 4.0, ALU.mult,
                                            ALU.mult).then_inc(out_scale_made, 1)
                elif name == "ternary":
                    dve.wait_ge(halves_made, 2)
                    dve.wait_ge(abs_summed, 3)
                    if j:
                        dve.wait_ge(tern_made, j)
                    nc.vector.tensor_scalar(tern_neg[:], w_ffn[j][:], half_neg[:, j:j + 1], None, ALU.is_lt
                                            ).then_inc(tern_neg_made, 1)
                    dve.wait_ge(tern_neg_made, j + 1)
                    nc.vector.scalar_tensor_tensor(w_tern[j][:], w_ffn[j][:], half_pos[:, j:j + 1], tern_neg[:],
                                                   ALU.is_gt, ALU.subtract).then_inc(tern_made, 1)
                elif name == "w_lo":
                    dve.wait_ge(w_hi_made, 1)
                    nc.vector.tensor_tensor(w_qkv_lo[:], w_qkv[:], w_qkv_hi[:].bitcast(F32), ALU.subtract
                                            ).then_inc(w_lo_made, 1)
                elif name.startswith("stats"):
                    k = int(name[-1]) - 1
                    dve.wait_ge(*((x_loaded[b], 16), (x1_made, b + 1), (x2_made, b + 1))[k])
                    for i in range(TT):
                        nc.vector.bn_stats(stats[k][:, i], x[:, b, i]).then_inc(stats_made[k], 1)
                    dve.wait_ge(stats_made[k], TT * (b + 1))
                    for i in range(TT):
                        nc.vector.bn_aggr(mean_var[k][:, i], stats[k][:, i]).then_inc(moments_made[k], 1)
                    dve.wait_ge(moments_made[k], TT * (b + 1))
                    nc.vector.tensor_scalar(var_eps[k][:], mean_var[k][:, :, 1], EPS_LN, None, ALU.add
                                            ).then_inc(var_made[k], 1)
                elif name.startswith("apply"):
                    k = int(name[-1]) - 1
                    dve.wait_ge(rstd_made[k], b + 1)
                    if b:
                        dve.wait_ge(turned_ln[k], b)
                    for i in range(TT):
                        nc.vector.tensor_scalar(xn[k][:, i], x[:, b, i], mean_var[k][:, i, 0:1], rstd[k][:, i:i + 1],
                                                ALU.subtract, ALU.mult).then_inc(normed[k], 1)
                elif name == "ln_lo1":
                    dve.wait_ge(lnT_hi[0], b + 1)
                    nc.vector.tensor_tensor(xT_lo[:], bank_of("ln_turn1", b, 0)[:].rearrange("p (k t) -> p k t", k=CT),
                                            xT_hi[:].bitcast(F32), ALU.subtract).then_inc(lnT_lo[0], 1)
                elif name == "ln_lo3":
                    dve.wait_ge(lnT_hi[2], b + 1)
                    nc.vector.tensor_tensor(x3T[:, 1], bank_of("ln_turn3", b, 0)[:].rearrange("p (k t) -> p k t", k=CT),
                                            x3T[:, 0], ALU.subtract).then_inc(lnT_lo[2], 1)
                elif name == "rotate":
                    n = 2 * b + j
                    bank = bank_of("qk", b, j)
                    dve.wait_ge(qk_projected, n + 1)
                    if b:
                        dve.wait_ge(qk_rotated, n - 1)
                        dve.wait_ge(qk_hi, n - 1)
                        dve.wait_ge(qk_lo, n - 1)
                    nc.vector.stream_shuffle(swapped[j][:].rearrange("p k t -> p (k t)"), bank[:],
                                             [i ^ 1 for i in range(32)]).then_inc(qk_swapped, 1)
                    nc.vector.tensor_tensor(turned[j][:], bank[:].rearrange("p (k t) -> p k t", k=CT),
                                            cos_t.rearrange("p (k t) -> p k t", k=1).broadcast_to((P, CT, T)),
                                            ALU.mult).then_inc(qk_cos, 1)
                elif name == "qk_lo":
                    dve.wait_ge(qk_hi, 2 * b + j + 1)
                    if b:
                        dve.wait_ge(scratch_written[j], 16 * b)
                    nc.vector.tensor_tensor(parts[j][:, 1], turned[j][:], parts[j][:, 0].bitcast(F32), ALU.subtract
                                            ).then_inc(qk_lo, 1)
                elif name == "sq_max":
                    dve.wait_ge(sq_made, SQ_STEPS * b + j + 1)
                    if j == 0 and b:
                        dve.wait_ge(max_lo, b)
                    if j < 4:
                        into, heads = neg_max[:, 0, 4 * j:4 * j + 4], 4
                    else:
                        into, heads = neg_max[:, 1, 2 * (j - 4):2 * (j - 4) + 2], 2
                    nc.vector.tensor_reduce(into, bank_of("sq", b, j)[:].rearrange("p (h k) -> p h k", h=heads), AX.X,
                                            ALU.max, negate=True).then_inc(sq_maxed, 1)
                elif name == "max_split":
                    dve.wait_ge(sq_maxed, SQ_STEPS * (b + 1))
                    if b:
                        dve.wait_ge(max_turned, b)
                    nc.vector.tensor_copy(max_parts[:, :, 0], neg_max[:]).then_inc(max_hi, 1)
                    dve.wait_ge(max_hi, b + 1)
                    nc.vector.tensor_tensor(max_parts[:, :, 1], neg_max[:], max_parts[:, :, 0].bitcast(F32),
                                            ALU.subtract).then_inc(max_lo, 1)
                elif name == "y_norm":
                    n = TT * b + j
                    dve.wait_ge(y_turned, n + 1)
                    dve.wait_ge(w_lo_made, 1)
                    if b:
                        dve.wait_ge(yn_turned, b)
                    bank = bank_of("y_turn", b, j)[:].rearrange("p (h d) -> p h d", d=32)
                    nc.vector.reciprocal(y_rec[:, j].rearrange("p (h a) -> p h a", a=1), bank[:, :, D:D + 1]
                                         ).then_inc(y_rec_made, 1)
                    dve.wait_ge(y_rec_made, n + 1)
                    nc.vector.tensor_tensor(yn[:, j].rearrange("p (h d) -> p h d", d=D), bank[:, :, 0:D],
                                            y_rec[:, j].rearrange("p (h a) -> p h a", a=1).broadcast_to((P, H, D)),
                                            ALU.mult).then_inc(y_normed, 1)
                elif name == "add1":
                    dve.wait_ge(projected, b + 1)
                    nc.vector.tensor_tensor(x[:, b], bank_of("proj", b, 0)[:].rearrange("p (i c) -> p i c", i=TT),
                                            x[:, b], ALU.add).then_inc(x1_made, 1)
                elif name == "add2":
                    dve.wait_ge(crossed, b + 1)
                    nc.vector.tensor_tensor(x[:, b], bank_of("cross", b, 0)[:].rearrange("p (i c) -> p i c", i=TT),
                                            x[:, b], ALU.add).then_inc(x2_made, 1)
                elif name == "ctx_max":
                    dve.wait_ge(ctx_scored, b + 1)
                    if b:
                        dve.wait_ge(ctx_exped, TT * b)
                    nc.vector.tensor_reduce(ctx_negmax[:], bank_of("ctx_scores", b, 0)[:].rearrange(
                        "p (i n) -> p i n", i=TT), AX.X, ALU.max, negate=True).then_inc(ctx_maxed, 1)
                elif name == "ctx_norm":
                    dve.wait_ge(ctx_exped, TT * (b + 1))
                    if b:
                        dve.wait_ge(ctx_turned, b)
                    nc.vector.reciprocal(ctx_rec[:], ctx_sum[:]).then_inc(ctx_rec_made, 1)
                    dve.wait_ge(ctx_rec_made, b + 1)
                    for i in range(TT):
                        nc.vector.tensor_scalar(ctx_attn[:, i], ctx_exp[:, i], ctx_rec[:, i:i + 1], None, ALU.mult
                                                ).then_inc(ctx_normed, 1)
                elif name == "act":
                    n = ET * b + j
                    dve.wait_ge(tanh_made, n + 1)
                    nc.vector.scalar_tensor_tensor(act_up[n % 2], tanh_up[n % 2], 1.0,
                                                   bank_of("up_gate", b, j)[:, 0:T], ALU.add, ALU.mult
                                                   ).then_inc(act_made, 1)
                elif name == "hidden":
                    n = ET * b + j
                    dve.wait_ge(act_made, n + 1)
                    if n >= 2:
                        dve.wait_ge(hid_hi, n - 1)
                        dve.wait_ge(hid_lo, n - 1)
                    nc.vector.scalar_tensor_tensor(hidden[n % 2], bank_of("up_gate", b, j)[:, T:2 * T], 0.125,
                                                   act_up[n % 2], ALU.mult, ALU.mult).then_inc(hidden_made, 1)
                elif name == "result":
                    dve.wait_ge(down_made, b + 1)
                    dve.wait_ge(out_scale_made, 2)
                    if b:
                        dve.wait_ge(stored, 16 * b)
                    nc.vector.scalar_tensor_tensor(
                        result.rearrange("p i c -> p (i c)"), bank_of("down", b, 0)[:],
                        out_scale[:, 1:2], x[:, b].rearrange("p i c -> p (i c)"), ALU.mult, ALU.add
                    ).then_inc(result_made, 1)

        @block.tensor
        def _(pe):
            def turn(dst, src, signal):
                for i in range(TT):
                    for k in range(CT):
                        last = nc.tensor.transpose(dst[:, k * T + i * P:k * T + (i + 1) * P],
                                                   src[:, i, k * P:(k + 1) * P], ident)
                last.then_inc(signal, 1)

            for name, b, j in ORDER[PE]:
                bank = free_bank(pe, name, b, j) if not (name == "pv" and j % 2) else bank_of(name, b, j)
                if name == "abs_total":
                    pe.wait_ge(ones_set, 1)
                    pe.wait_ge(abs_summed, 3)
                    nc.tensor.matmul(bank[:, 0:3], ones[:], abs_sum[:], start=True, stop=True
                                     ).then_inc(abs_total, 1)
                elif name.startswith("ln_turn"):
                    k = int(name[-1]) - 1
                    pe.wait_ge(normed[k], TT * (b + 1))
                    pe.wait_ge(consts_loaded, 16)
                    turn(bank, xn[k], turned_ln[k])
                elif name == "qk":
                    pe.wait_ge(lnT_lo[0], b + 1)
                    pe.wait_ge(w_lo_made, 1)
                    for m in range(CT):
                        terms = [(k, w, a) for k in range(CT) for w, a in
                                 ((w_qkv_hi, xT_hi), (w_qkv_hi, xT_lo), (w_qkv_lo, xT_hi))]
                        for t, (k, w, a) in enumerate(terms):
                            last = nc.tensor.matmul(bank[:, m * T:(m + 1) * T],
                                                    w[:, k, j * C + m * P:j * C + (m + 1) * P], a[:, k, :],
                                                    start=(t == 0), stop=(t == len(terms) - 1))
                    last.then_inc(qk_projected, 1)
                elif name == "v":
                    for i in range(TT):
                        terms = [(k, w, a) for k in range(CT) for w, a in
                                 ((w_qkv_hi, xT_hi), (w_qkv_hi, xT_lo), (w_qkv_lo, xT_hi))]
                        for t, (k, w, a) in enumerate(terms):
                            last = nc.tensor.matmul(bank[:, i * C:(i + 1) * C], a[:, k, i * P:(i + 1) * P],
                                                    w[:, k, 2 * C:3 * C], start=(t == 0), stop=(t == len(terms) - 1))
                    last.then_inc(v_projected, 1)
                elif name == "sq":
                    n = SQ_STEPS * b + j
                    q, k = pack[0][b % 2], pack[1][b % 2]
                    if j == 0:
                        pe.wait_ge(ident16_made, 1)
                        pe.wait_ge(mask_made, 1)
                        pe.wait_ge(pack_rows_set, 3)
                        pe.wait_ge(key_rows_set, 1)
                        for s in range(2):
                            pe.wait_ge(packed[s][b % 2], 16 * TERMS * (b // 2 + 1))
                    if j < 4:
                        nc.tensor.matmul(bank[:], ident16[:], mask16[:].rearrange("p a k -> p (a k)"), start=True,
                                         stop=False, skip_group_check=True)
                        for a in range(4):
                            h = 4 * j + a
                            last = nc.tensor.matmul(bank[:, a * P:(a + 1) * P], q[0:MROW, h, 0:P], k[0:MROW, h, 0:P],
                                                    start=False, stop=(a == 3), skip_group_check=True)
                    else:
                        nc.tensor.matmul(bank[:].rearrange("p (h k) -> p h k", h=2)[:, :, P:T], ident16[:],
                                         mask16[:, 0:2, :], start=True, stop=False, skip_group_check=True)
                        for a in range(2):
                            h = 2 * (j - 4) + a
                            last = nc.tensor.matmul(bank[:, a * T:(a + 1) * T], q[0:MROW, h, P:T], k[0:MROW, h, :],
                                                    start=False, stop=(a == 1), skip_group_check=True)
                    last.then_inc(sq_made, 1)
                elif name == "max_turn":
                    pe.wait_ge(max_lo, b + 1)
                    for i in range(TT):
                        last = nc.tensor.transpose(bank[0:32, i * P:(i + 1) * P],
                                                   max_parts[:, i].rearrange("p a h -> p (a h)").bitcast(F32), ident)
                    last.then_inc(max_turned, 1)
                elif name == "st":
                    n = ST_STEPS * b + j
                    q, k = pack[0][b % 2], pack[1][b % 2]
                    if j == 0:
                        pe.wait_ge(max_placed[b % 2], 32 * (b // 2 + 1))
                    g, u = j // 3, j % 3
                    K = MROW + ONES_ROW
                    if u < 2:
                        for a in range(2):
                            h = 4 * g + 2 * u + a
                            last = nc.tensor.matmul(bank[:, a * T:(a + 1) * T], k[0:K, h, 0:P], q[0:K, h, :],
                                                    start=True, stop=True)
                    else:
                        for a in range(4):
                            h = 4 * g + a
                            last = nc.tensor.matmul(bank[:, a * P:(a + 1) * P], k[0:K, h, P:T], q[0:K, h, P:T],
                                                    start=True, stop=True)
                    last.then_inc(st_made, 1)
                elif name == "pv":
                    n = G * b + j
                    pe.wait_ge(probs_masked, 2 * (n + 1))
                    if j == 0:
                        pe.wait_ge(v_stored, b + 1)
                    pr, va, off = probs[n % 2], v_aug[b % 2], (j % 2) * T
                    for a in range(4):
                        nc.tensor.matmul(bank[32 * a:32 * a + 32, off:off + T], va[:, 0, 4 * j + a, :],
                                         pr[:, a // 2, (a % 2) * T:(a % 2) * T + T], start=True, stop=False,
                                         skip_group_check=True)
                    for a in range(4):
                        last = nc.tensor.matmul(bank[32 * a:32 * a + 32, off + P:off + T], va[:, 1, 4 * j + a, :],
                                                pr[:, 2, a * P:(a + 1) * P], start=False, stop=True,
                                                skip_group_check=True)
                    last.then_inc(pv_made, 1)
                elif name == "y_turn":
                    pe.wait_ge(y_stored, 2 * (b + 1))
                    for g in range(G):
                        last = nc.tensor.transpose(bank[:, g * P:(g + 1) * P], yT_raw[:, g, j * P:(j + 1) * P],
                                                   ident)
                    last.then_inc(y_turned, 1)
                elif name == "yn_turn":
                    pe.wait_ge(y_normed, TT * (b + 1))
                    turn(bank, yn, yn_turned)
                elif name == "proj":
                    pe.wait_ge(ynT_stored, b + 1)
                    pe.wait_ge(wproj_loaded, 16)
                    for i in range(TT):
                        for k in range(CT):
                            last = nc.tensor.matmul(bank[:, i * C:(i + 1) * C], ynT[:, k, i * P:(i + 1) * P],
                                                    w_proj[:, k, :], start=(k == 0), stop=(k == CT - 1))
                    last.then_inc(projected, 1)
                elif name == "cross":
                    pe.wait_ge(lnT_hi[1], b + 1)
                    pe.wait_ge(attnT_stored, b + 1)
                    for i in range(TT):
                        for k in range(CT):
                            last = nc.tensor.matmul(bank[:, i * C:(i + 1) * C], x2T[:, k, i * P:(i + 1) * P],
                                                    attnT[b % 2][:, k, :], start=(k == 0), stop=(k == CT - 1))
                    last.then_inc(crossed, 1)
                elif name == "ctx_qk":
                    pe.wait_ge(ctx_loaded, 48)
                    for a in range(2):
                        last = nc.tensor.matmul(bank[:, a * T:(a + 1) * T], w_ctx[:, a, :], ctxT[:, b, :],
                                                start=True, stop=True)
                    last.then_inc(ctx_projected, 1)
                elif name == "ctx_scores":
                    pe.wait_ge(ctx_qk_made, 2 * (b + 1))
                    for i in range(TT):
                        last = nc.tensor.matmul(bank[:, i * T:(i + 1) * T], ctx_qk[:, 0, i * P:(i + 1) * P],
                                                ctx_qk[:, 1, :], start=True, stop=True)
                    last.then_inc(ctx_scored, 1)
                elif name == "ctx_turn":
                    pe.wait_ge(ctx_normed, TT * (b + 1))
                    turn(bank, ctx_attn, ctx_turned)
                elif name == "up_gate":
                    if j == 0:
                        pe.wait_ge(lnT_lo[2], b + 1)
                        pe.wait_ge(tern_made, 2)
                    for w in range(2):
                        wt = w_tern[w][:].rearrange("p (k n) -> p k n", k=CT)
                        for t in range(2 * CT):
                            last = nc.tensor.matmul(bank[:, w * T:(w + 1) * T], wt[:, t // 2, j * P:(j + 1) * P],
                                                    x3T[:, t % 2, t // 2, :], start=(t == 0), stop=(t == 2 * CT - 1))
                    last.then_inc(up_gate_made, 1)
                elif name == "down":
                    pe.wait_ge(hid_lo, ET * (b + 1))
                    pe.wait_ge(tern_made, 3)
                    wt = w_tern[2][:].rearrange("p (k n) -> p k n", k=ET)
                    for i in range(TT):
                        for t in range(2 * ET):
                            last = nc.tensor.matmul(bank[:, i * C:(i + 1) * C], hid[:, t % 2, t // 2, i * P:(i + 1) * P],
                                                    wt[:, t // 2, :], start=(t == 0), stop=(t == 2 * ET - 1))
                    last.then_inc(down_made, 1)


def constants():
    theta = (1.0 / 10000.0 ** (np.arange(0, D, 2, dtype=np.float32) / np.float32(D))).astype(np.float32)
    angle = np.outer(np.arange(T, dtype=np.float32), theta).astype(np.float32)
    channel = np.arange(P) % D
    cos = np.cos(angle).astype(np.float32)[:, channel // 2].T
    sin = np.sin(angle).astype(np.float32)[:, channel // 2].T
    sin = sin * np.where(channel % 2 == 0, -1.0, 1.0).astype(np.float32)[:, None]
    return np.ascontiguousarray(np.concatenate([np.eye(P, dtype=np.float32), cos, sin], axis=1))


def kernel(**inputs):
    import concourse.bacc as bacc
    from concourse.bass_utils import run_bass_kernel_spmd

    a = {k: np.asarray(v) for k, v in inputs.items()}
    arrays = {
        "x": a["x"],
        "ctxT": a["ctx_1024"].transpose(0, 2, 1),
        "wqkvT": a["L0_attn_w_atten"].T,
        "wpT": a["L0_attn_w_proj"].T,
        "wctxT": np.stack([a["L0_xattn_Wq"].T, a["L0_xattn_Wk"].T]),
        "bctx": np.stack([a["L0_xattn_bq"], a["L0_xattn_bk"]], axis=1),
        "wupT": a["L0_ffn_W_up"].T,
        "wgateT": a["L0_ffn_W_gate"].T,
        "wdownT": a["L0_ffn_W_down"].T,
        "consts": constants(),
    }
    arrays = {f"in_{k}": np.ascontiguousarray(v) for k, v in arrays.items()}
    nc = bacc.Bacc("TRN2", target_bir_lowering=False, num_devices=1)
    args = [nc.dram_tensor(k, v.shape, mybir.dt.from_np(v.dtype), kind="ExternalInput").ap() for k, v in arrays.items()]
    out = nc.dram_tensor("out", (B, T, C), F32, kind="ExternalOutput").ap()
    decoder_kernel(nc, *args, out)
    r = run_bass_kernel_spmd(nc, [arrays], core_ids=[0])
    return r.results[0]["out"]
```

```python
from contextlib import ExitStack

import numpy as np

import concourse.bass as bass
from concourse import mybir

F32 = mybir.dt.float32
F32R = mybir.dt.float32r
F16 = mybir.dt.float16
BF16 = mybir.dt.bfloat16
ALU = mybir.AluOpType
ACT = mybir.ActivationFunctionType
AX = mybir.AxisListType

P = 128
B = 4
T = 256
C = 256
H = 16
D = C // H
E = 1024
DX = 128
TT = T // P
CT = C // P
ET = E // P
EP = ET // 2
RING = 3
G = H // 4
TERMS = 4
MROW = 96
MAX_PARTS = 2
EPS_LN = 1e-5
EPS_Q = 1e-8
MASKED = -1e30
WARM_UP = 14
PACK_DMAS = 6
HALF = H // CT
SQ_HALF = HALF // 4 + HALF // 2
SQ_STEPS = CT * SQ_HALF
ST_STEPS = 3 * G
ST_HALF = ST_STEPS // CT


PE, DVE, ACTE, POOL, SP = "tensor", "vector", "scalar", "gpsimd", "sync"
SEMAPHORE_NS = 220
COUNT = {"qk": CT, "rotate": CT, "rotate_add": CT, "qk_hi": CT, "qk_lo": CT, "pack_hi": CT, "pack_lo": CT,
         "sq": SQ_STEPS, "sq_max": SQ_STEPS, "max_split": CT, "max_turn": CT, "max_store": CT, "max_rows": CT,
         "st": ST_STEPS, "exp": ST_STEPS, "mask": G, "pv": G, "y_store": CT, "y_turn": TT, "y_norm": TT,
         "up": EP, "gate": EP, "tanh": EP, "act": EP, "hidden": EP, "hid_hi": EP, "hid_lo": EP,
         "down": EP, "result": TT, "store": TT}
PARTS = {
    "ctx_qk": (PE, 860), "ctx_bias": (ACTE, 700), "ctx_scores": (PE, 860), "ctx_max": (DVE, 600),
    "ctx_exp": (ACTE, 900), "ctx_norm": (DVE, 700), "ctx_turn": (PE, 430), "ctx_store": (ACTE, 480),
    "stats1": (DVE, 1320), "stats2": (DVE, 1320), "stats3": (DVE, 1320),
    "rstd1": (POOL, 850), "rstd2": (POOL, 850), "rstd3": (POOL, 850),
    "apply1": (ACTE, 980), "apply2": (ACTE, 980), "apply3": (ACTE, 980),
    "ln_turn1": (PE, 430), "ln_turn2": (PE, 430), "ln_turn3": (PE, 430),
    "ln_hi1": (ACTE, 480), "ln_hi2": (ACTE, 480), "ln_hi3": (ACTE, 480), "ln_lo1": (DVE, 600), "ln_lo3": (DVE, 600),
    "qk": (PE, 1310), "rotate": (DVE, 1200), "rotate_add": (POOL, 2700), "qk_hi": (ACTE, 520), "qk_lo": (POOL, 1230),
    "pack_hi": (SP, 1970), "pack_lo": (SP, 1970), "v": (PE, 1310), "v_store": (ACTE, 480),
    "sq": (PE, 330), "sq_max": (DVE, 600), "max_split": (DVE, 350), "max_turn": (PE, 200), "max_store": (ACTE, 270),
    "max_rows": (SP, 650), "st": (PE, 230), "exp": (ACTE, 480), "mask": (POOL, 1200), "pv": (PE, 780),
    "y_store": (ACTE, 480), "y_turn": (PE, 430), "y_norm": (DVE, 620), "yn_turn": (PE, 430), "yn_store": (ACTE, 480),
    "proj": (PE, 1720), "add1": (DVE, 600), "cross": (PE, 1720), "add2": (DVE, 600),
    "up": (PE, 870), "gate": (PE, 870), "tanh": (ACTE, 580), "act": (DVE, 600), "hidden": (DVE, 600),
    "hid_hi": (ACTE, 520), "hid_lo": (POOL, 1120), "down": (PE, 870), "result": (DVE, 400), "store": (SP, 480),
    "w_hi": (ACTE, 520), "w_lo": (DVE, 600), "abs": (ACTE, 1900), "abs_total": (PE, 500), "scales": (DVE, 700),
    "below": (DVE, 1150), "ternary": (DVE, 2270), "pad": (POOL, 1740), "pad_copy": (SP, 480),
}
ONCE = {"w_hi": 3, "w_lo": 3, "abs": 3, "abs_total": 1, "scales": 1, "below": 3, "ternary": 3, "pad": 4, "pad_copy": 1}
ARRIVAL_NS = {("stats1", 0, 0): 3400, ("ctx_qk", 0, 0): 5100, ("w_hi", 0, 0): 6700, ("w_hi", 0, 1): 7400,
              ("w_hi", 0, 2): 7700, ("stats1", 1, 0): 8700, ("ctx_qk", 2, 0): 9400, ("abs", 0, 0): 12400,
              ("abs", 0, 1): 15300, ("abs", 0, 2): 18200, ("stats1", 2, 0): 18900, ("proj", 0, 0): 19700,
              ("stats1", 3, 0): 20400}
EXTRA_NS = {"pack_hi": 1900, "pack_lo": 1900, "max_rows": 1650, "store": 1700, "pad_copy": 4700}
FREED_BY = {"ctx_qk": "ctx_bias", "ctx_scores": "ctx_exp", "ctx_turn": "ctx_store", "ln_turn1": "ln_lo1",
            "ln_turn2": "ln_hi2", "ln_turn3": "ln_lo3", "qk": "rotate", "v": "v_store", "sq": "sq_max",
            "max_turn": "max_store", "st": "exp", "y_turn": "y_norm", "yn_turn": "yn_store", "proj": "add1",
            "cross": "add2", "up": "act", "gate": "hidden", "down": "result", "abs_total": "scales", "pv": "y_store"}

START_NS = {POOL: 3100, ACTE: 3900, DVE: 900, SP: 8000}
SHIFT_NS = {
    "abs": 380000, "abs_total": -106000, "act": 180000, "add1": -4000, "add2": 78000, "apply1": -350000,
    "apply2": 132000, "apply3": -20000, "below": 214000, "cross": -68000, "ctx_bias": 120000, "ctx_exp": -90000,
    "ctx_max": 82000, "ctx_norm": -156000, "ctx_qk": -252000, "ctx_scores": -14000, "ctx_store": 204000,
    "ctx_turn": 308000, "down": 254000, "exp": -66000, "gate": 26000, "hid_hi": 152000, "hid_lo": 82000,
    "hidden": -178000, "ln_hi1": -118000, "ln_hi2": -242000, "ln_hi3": -224000, "ln_lo1": -320000, "ln_lo3":
    224000, "ln_turn1": 114000, "ln_turn3": 132000, "mask": -134000, "max_rows": 4000, "max_split": -240000,
    "max_store": 114000, "max_turn": 70000, "pack_hi": 94000, "pack_lo": -318000, "pad": 170000, "pad_copy":
    -10000, "proj": 72000, "pv": 2000, "qk": -40000, "qk_hi": -390000, "qk_lo": 38000, "result": 292000,
    "rotate": -128000, "rotate_add": 272000, "rstd1": -192000, "rstd2": -242000, "rstd3": -212000, "scales":
    408000, "sq": 150000, "sq_max": -136000, "st": -16000, "stats1": -72000, "stats2": -280000, "stats3": 4000,
    "store": -122000, "tanh": -106000, "ternary": 26000, "up": 16000, "v": 132000, "v_store": 160000, "w_hi":
    -182000, "w_lo": 338000, "y_norm": -158000, "y_store": -420000, "y_turn": -210000, "yn_store": -256000,
    "yn_turn": 64000}
BATCH_NS = (0, -8000, -120000, -92000)

SHARED = {"pv": 2, "down": EP}
LAST_FREEING = {"down": lambda j: TT - 1, "pv": lambda j: j // 2}


def needs(name, b, j):
    def n(other, k, count):
        return (other, k // count, k % count)

    table = {
        "ctx_bias": [("ctx_qk", b, 0), ("ctx_scores", b - 1, 0)],
        "ctx_scores": [("ctx_bias", b, 0)],
        "ctx_max": [("ctx_scores", b, 0), ("ctx_exp", b - 1, 0)],
        "ctx_exp": [("ctx_max", b, 0), ("ctx_norm", b - 1, 0)],
        "ctx_norm": [("ctx_exp", b, 0), ("ctx_turn", b - 1, 0)],
        "ctx_turn": [("ctx_norm", b, 0)],
        "ctx_store": [("ctx_turn", b, 0), ("cross", b - 2, 0)],
        "stats1": [],
        "stats2": [("add1", b, 0)],
        "stats3": [("add2", b, 0)],
        "ln_hi1": [("ln_turn1", b, 0), ("v", b - 1, 0), ("qk", b - 1, 1), ("ln_lo1", b - 1, 0)],
        "ln_hi2": [("ln_turn2", b, 0), ("cross", b - 1, 0)],
        "ln_hi3": [("ln_turn3", b, 0), ("gate", b - 1, EP - 1), ("ln_lo3", b - 1, 0), ("ternary", 0, 2)],
        "ln_lo1": [("ln_hi1", b, 0)],
        "ln_lo3": [("ln_hi3", b, 0)],
        "w_lo": [("w_hi", 0, j)],
        "qk": [("ln_lo1", b, 0), ("w_lo", 0, j)],
        "rotate": [("qk", b, j), ("rotate_add", b - 1, j), ("qk_hi", b - 1, j), ("qk_lo", b - 1, j)],
        "rotate_add": [("rotate", b, j)],
        "qk_hi": [("rotate_add", b, j), ("pack_lo", b - 1, j)],
        "qk_lo": [("qk_hi", b, j)],
        "pack_hi": [("qk_hi", b, j), ("pad", 0, 2 * j + 1), ("st", b - 2, ST_HALF * (j + 1) - 1)],
        "pack_lo": [("qk_lo", b, j), ("pack_hi", b, j)],
        "v": [("ln_lo1", b, 0), ("w_lo", 0, 2)],
        "v_store": [("v", b, 0), ("pv", b - 2, G - 1)],
        "sq": [("pack_lo", b, j // SQ_HALF), ("w_lo", 0, 0)] + [("pad_copy", 0, 0)] * (b % 2),
        "pad_copy": [("pad", 0, 3)],
        "sq_max": [("sq", b, j), ("max_split", b - 1, j // SQ_HALF)],
        "max_split": [("sq_max", b, SQ_HALF * (j + 1) - 1), ("max_turn", b - 1, j)],
        "max_turn": [("max_split", b, j)],
        "max_store": [("max_turn", b, j), ("max_rows", b - 1, j)],
        "max_rows": [("max_store", b, j), ("pad_copy", 0, 0)],
        "st": [("max_rows", b, j // ST_HALF)],
        "exp": [("st", b, j), n("pv", G * b + j // 3 - 2, G)],
        "mask": [("exp", b, 3 * j + 2)],
        "pv": [("mask", b, j), ("v_store", b, 0)],
        "y_store": [("pv", b, 2 * j + 1), ("y_turn", b - 1, TT - 1), ("w_lo", 0, 2)],
        "y_turn": [("y_store", b, 1)],
        "y_norm": [("y_turn", b, j), ("yn_turn", b - 1, 0), ("w_lo", 0, 2)],
        "yn_turn": [("y_norm", b, TT - 1)],
        "yn_store": [("yn_turn", b, 0), ("proj", b - 1, 0)],
        "proj": [("yn_store", b, 0)],
        "add1": [("proj", b, 0)],
        "cross": [("ln_hi2", b, 0), ("ctx_store", b, 0)],
        "add2": [("cross", b, 0)],
        "abs": [],
        "abs_total": [("abs", 0, 2)],
        "scales": [("abs_total", 0, 0)],
        "below": [("scales", 0, 0), ("abs", 0, 2), ("ternary", 0, j - 1 if j else -1)],
        "ternary": [("below", 0, j)],
        "up": [("ln_lo3", b, 0), ("ternary", 0, 0)],
        "gate": [("ln_lo3", b, 0), ("ternary", 0, 1)],
        "tanh": [("up", b, j), n("hid_lo", EP * b + j - RING, EP), ("ternary", 0, 1)],
        "act": [("tanh", b, j)],
        "hidden": [("act", b, j), ("gate", b, j)],
        "hid_hi": [("hidden", b, j), ("down", b - 1, j)],
        "hid_lo": [("hid_hi", b, j)],
        "down": [("hid_lo", b, j), ("ternary", 0, 2)],
        "result": [("down", b, EP - 1), ("store", b - 1, j), ("ternary", 0, 1)],
        "store": [("result", b, j)],
    }
    for k in "123":
        table["stats" + k] = table["stats" + k] + [("rstd" + k, b - 1, 0)]
        table["rstd" + k] = [("stats" + k, b, 0), ("apply" + k, b - 1, 0)]
        table["apply" + k] = [("rstd" + k, b, 0), ("ln_turn" + k, b - 1, 0)] + [("ternary", 0, 2)] * (k == "3")
        table["ln_turn" + k] = [("apply" + k, b, 0)]
    found = [x for x in table.get(name, []) if x[1] >= 0 and x[2] >= 0]
    count = ONCE.get(name) or COUNT.get(name, 1)
    before = b * count + j - 1
    if before >= 0:
        found.append((name, before // count, before % count))
    return found


def plan(batch_ns=BATCH_NS, urgency=0.001, shift=SHIFT_NS, banks=8):
    every = [(name, b, j) for name in PARTS for b in range(1 if name in ONCE else B)
             for j in range(ONCE.get(name) or COUNT.get(name, 1))]
    before_it = {part: needs(*part) for part in every}
    after_it = {part: [] for part in every}
    for part in every:
        for x in before_it[part]:
            after_it[x].append(part)
    alone = {}

    def nominal(part):
        name, b, j = part
        if part not in alone:
            alone[part] = max([nominal(x) + PARTS[x[0]][1] + (x[0] != name) * (EXTRA_NS.get(x[0], 0) + SEMAPHORE_NS)
                               for x in before_it[part]] + [batch_ns[b]])
        return alone[part]

    ends, order, bank_of, before = {}, {e: [] for e in (PE, DVE, ACTE, POOL, SP)}, {}, {}
    engine_free = {e: START_NS.get(e, 0) for e in order}
    bank_free, bank_last, freeing = [0] * banks, [None] * banks, {}
    missing = {part: len(before_it[part]) for part in every}
    rank = {part: urgency * (nominal(part) + shift.get(part[0], 0)) for part in every}
    ready_at = {part: ARRIVAL_NS.get(part, 0) for part in every}
    candidates = sorted([part for part in every if not missing[part]], key=rank.get)
    while candidates:
        best = None
        for part in candidates:
            name, b, j = part
            start = max(engine_free[PARTS[name][0]], ready_at[part])
            if name in FREED_BY and j % SHARED.get(name, 1) == 0:
                if min(bank_free) == float("inf"):
                    continue
                start = max(start, min(bank_free) + SEMAPHORE_NS)
            score = start + rank[part]
            if best is None or score < best[0]:
                best = (score, start, part)
        _, start, part = best
        name, b, j = part
        candidates.remove(part)
        engine, ns = PARTS[name]
        order[engine].append(part)
        engine_free[engine] = start + ns
        ends[part] = start + ns + EXTRA_NS.get(name, 0)
        if j % SHARED.get(name, 1):
            bank_of[part] = bank_of[name, b, j - 1]
        elif name in FREED_BY:
            ready = [i for i in range(banks) if bank_free[i] + SEMAPHORE_NS <= start]
            bank = min(ready or range(banks), key=lambda i: bank_free[i])
            bank_of[part], before[part] = bank, bank_last[bank]
            bank_last[bank], bank_free[bank] = part, float("inf")
            freeing[FREED_BY[name], b, LAST_FREEING.get(name, int)(j)] = bank
        if part in freeing:
            bank_free[freeing[part]] = ends[part]
        for x in after_it[part]:
            if x[0] != name:
                ready_at[x] = max(ready_at[x], ends[part] + SEMAPHORE_NS)
            missing[x] -= 1
            if not missing[x]:
                candidates.append(x)
    return order, bank_of, before


def decoder_kernel(nc, x_in, ctxT_in, wqkvT_in, wpT_in, wctxT_in, bctx_in, wupT_in, wgateT_in, wdownT_in,
                   consts_in, out):
    ORDER, BANK, BANK_BEFORE = plan()

    with ExitStack() as ctx:
        def sb(name, shape, dt=F32):
            return ctx.enter_context(nc.sbuf_tensor(name, shape, dt))

        def psum(name, shape):
            return ctx.enter_context(nc.psum_tensor(name, shape, F32))

        def sem(name):
            return ctx.enter_context(nc.semaphore(name))

        banks = [psum(f"bank{i}", [P, 512]) for i in range(8)]

        def w_third(w, j):
            if j == CT:
                return w[:, :, 2 * C:3 * C].rearrange("p k (s c) -> p k s c", s=2)
            return w[:, :, 0:2 * C].rearrange("p k (s m c) -> p k s m c", s=2, m=CT)[:, :, :, j]

        def bank_of(name, b, j):
            return banks[BANK[name, b, j]]

        x = sb("x", [P, B, TT, C])
        w_qkv = sb("w_qkv", [P, CT, 3 * C])
        w_qkv_hi = sb("w_qkv_hi", [P, CT, 3 * C], F32R)
        w_qkv_lo = sb("w_qkv_lo", [P, CT, 3 * C], F32R)
        w_proj = sb("w_proj", [P, CT, C])
        w_ctx = sb("w_ctx", [P, 2, DX])
        b_ctx = sb("b_ctx", [P, 2])
        w_ffn = [sb(f"w_ffn{k}", [P, 2048]) for k in range(3)]
        w_tern = [sb(f"w_tern{k}", [P, 2048], F16) for k in range(3)]
        tern_neg = sb("tern_neg", [P, 2048], F16)
        abs_sum = sb("abs_sum", [P, 3])
        scales = sb("scales", [P, 3])
        half_pos = sb("half_pos", [P, 3])
        half_neg = sb("half_neg", [P, 3])
        out_scale = sb("out_scale", [P, 2])
        consts = sb("consts", [P, P + 2 * T])
        ident = consts[:, 0:P]
        cos_t, sin_t = consts[:, P:P + T], consts[:, P + T:P + 2 * T]
        ident16 = sb("ident16", [P, P], BF16)
        mask16 = sb("mask16", [P, 4, P], BF16)
        ones = sb("ones", [P, P])
        neg_half = sb("neg_half", [P, TT])

        stats = [sb(f"stats{k}", [P, TT, 6]) for k in (1, 2, 3)]
        mean_var = [sb(f"mean_var{k}", [P, TT, 2]) for k in (1, 2, 3)]
        var_eps = [sb(f"var_eps{k}", [P, TT]) for k in (1, 2, 3)]
        neg_mean = [sb(f"neg_mean{k}", [P, TT]) for k in (1, 2, 3)]
        rstd = [sb(f"rstd{k}", [P, TT]) for k in (1, 2, 3)]
        ln_bias = [sb(f"ln_bias{k}", [P, TT]) for k in (1, 2, 3)]
        spare_down = w_ffn[2][:].rearrange("p (n t) -> p n t", t=T)
        xn = [sb("xn1", [P, TT, C]), sb("xn2", [P, TT, C]), spare_down[:, 0:2]]
        xT_hi = sb("xT_hi", [P, CT, T], F32R)
        xT_lo = sb("xT_lo", [P, CT, T], F32R)
        x2T = sb("x2T", [P, CT, T])
        x3T = spare_down[:, 2:4].bitcast(F16).rearrange("p n (k t) -> p n k t", k=CT)

        swapped = [sb(f"swapped{m}", [P, 2, T]) for m in range(CT)]
        turned = [sb(f"turned{m}", [P, 2, T]) for m in range(CT)]
        parts = [sb(f"parts{m}", [P, 2, 2, T], F32R) for m in range(CT)]
        pack = [sb(f"pack{i}", [P, H, 2, T], F32R) for i in range(2)]
        v_aug = [sb(f"v_aug{i}", [P, TT, H, 32]) for i in range(2)]
        neg_max = [sb(f"neg_max{m}", [P, TT, HALF]) for m in range(CT)]
        max_parts = [sb(f"max_parts{m}", [P, TT, 2, HALF], F32R) for m in range(CT)]
        maxT = [sb(f"maxT{m}", [2 * HALF, T]) for m in range(CT)]
        probs = [sb(f"probs{i}", [P, 3, 512]) for i in range(2)]
        spare_qkv = w_qkv[:].rearrange("p k n -> p (k n)").rearrange("p (n t) -> p n t", t=T)
        yT_raw = spare_qkv[:, 0:G]
        y_rec = sb("y_rec", [P, TT, H])
        yn = spare_qkv[:, G:G + TT]
        ynT = sb("ynT", [P, CT, T])

        ctxT = sb("ctxT", [P, B, T])
        ctx_qk = sb("ctx_qk", [P, 2, T])
        ctx_negmax = sb("ctx_negmax", [P, TT])
        ctx_sum = sb("ctx_sum", [P, TT])
        ctx_rec = sb("ctx_rec", [P, TT])
        ctx_exp = sb("ctx_exp", [P, TT, T])
        ctx_attn = sb("ctx_attn", [P, TT, T])
        attnT = [sb(f"attnT{i}", [P, CT, T]) for i in range(2)]

        spare = w_ffn[1][:].rearrange("p (n t) -> p n t", t=T)
        pair = [spare[:, 2 * i:2 * i + 2] for i in range(RING)]
        result = spare[:, 6:8]
        hid = w_ffn[0][:].bitcast(F16).rearrange("p (a m t) -> p a m t", a=2, m=ET)

        x_loaded = [sem(f"x_loaded{b}") for b in range(B)]
        wqkv_loaded = [sem(f"wqkv_loaded{j}") for j in range(3)]
        consts_loaded = sem("consts_loaded")
        ctx_loaded = [sem(f"ctx_loaded{i}") for i in range(2)]
        wproj_loaded = sem("wproj_loaded")
        ffn_loaded = [sem(f"ffn_loaded{k}") for k in range(3)]
        ones_set = sem("ones_set")
        neg_half_set = sem("neg_half_set")
        ident16_made = sem("ident16_made")
        mask_filled = sem("mask_filled")
        mask_made = sem("mask_made")
        pads_set = sem("pads_set")
        pads_copied = sem("pads_copied")
        v_ones_set = sem("v_ones_set")
        w_hi_made = sem("w_hi_made")
        w_lo_made = sem("w_lo_made")
        abs_summed = sem("abs_summed")
        abs_total = sem("abs_total")
        scales_made = sem("scales_made")
        halves_made = sem("halves_made")
        out_scale_made = sem("out_scale_made")
        below_made = sem("below_made")
        tern_made = sem("tern_made")
        stats_made = [sem(f"stats_made{k}") for k in (1, 2, 3)]
        moments_made = [sem(f"moments_made{k}") for k in (1, 2, 3)]
        var_made = [sem(f"var_made{k}") for k in (1, 2, 3)]
        neg_mean_made = [sem(f"neg_mean_made{k}") for k in (1, 2, 3)]
        ln_bias_made = [sem(f"ln_bias_made{k}") for k in (1, 2, 3)]
        rstd_made = [sem(f"rstd_made{k}") for k in (1, 2, 3)]
        normed = [sem(f"normed{k}") for k in (1, 2, 3)]
        turned_ln = [sem(f"turned_ln{k}") for k in (1, 2, 3)]
        lnT_hi = [sem(f"lnT_hi{k}") for k in (1, 2, 3)]
        lnT_lo = [sem(f"lnT_lo{k}") for k in (1, 2, 3)]
        qk_projected = sem("qk_projected")
        qk_swapped = sem("qk_swapped")
        qk_cos = sem("qk_cos")
        qk_sin = sem("qk_sin")
        qk_rotated = sem("qk_rotated")
        qk_hi = sem("qk_hi")
        qk_lo = sem("qk_lo")
        packed = [[sem(f"packed{m}{i}") for i in range(2)] for m in range(CT)]
        v_projected = sem("v_projected")
        v_stored = sem("v_stored")
        sq_made = sem("sq_made")
        sq_maxed = sem("sq_maxed")
        max_hi = sem("max_hi")
        max_lo = sem("max_lo")
        max_turned = sem("max_turned")
        maxT_made = sem("maxT_made")
        max_placed = [[sem(f"max_placed{m}{i}") for i in range(2)] for m in range(CT)]
        st_made = sem("st_made")
        exp_made = sem("exp_made")
        probs_masked = sem("probs_masked")
        pv_made = sem("pv_made")
        y_stored = sem("y_stored")
        y_turned = sem("y_turned")
        y_rec_made = sem("y_rec_made")
        y_normed = sem("y_normed")
        yn_turned = sem("yn_turned")
        ynT_stored = sem("ynT_stored")
        projected = sem("projected")
        x1_made = sem("x1_made")
        ctx_projected = sem("ctx_projected")
        ctx_qk_made = sem("ctx_qk_made")
        ctx_scored = sem("ctx_scored")
        ctx_maxed = sem("ctx_maxed")
        ctx_exped = sem("ctx_exped")
        ctx_rec_made = sem("ctx_rec_made")
        ctx_normed = sem("ctx_normed")
        ctx_turned = sem("ctx_turned")
        attnT_stored = sem("attnT_stored")
        crossed = sem("crossed")
        x2_made = sem("x2_made")
        up_made = sem("up_made")
        gate_made = sem("gate_made")
        tanh_made = sem("tanh_made")
        act_made = sem("act_made")
        hidden_made = sem("hidden_made")
        hid_hi = sem("hid_hi")
        hid_lo = sem("hid_lo")
        down_made = sem("down_made")
        result_made = sem("result_made")
        stored = [sem(f"stored{i}") for i in range(TT)]

        FREED = {
            "abs_total": lambda b, j: (scales_made, 1),
            "ln_turn1": lambda b, j: (lnT_lo[0], b + 1),
            "ln_turn2": lambda b, j: (lnT_hi[1], b + 1),
            "ln_turn3": lambda b, j: (lnT_lo[2], b + 1),
            "qk": lambda b, j: (qk_cos, 2 * b + j + 1),
            "v": lambda b, j: (v_stored, b + 1),
            "sq": lambda b, j: (sq_maxed, SQ_STEPS * b + j + 1),
            "max_turn": lambda b, j: (maxT_made, 2 * b + j + 1),
            "st": lambda b, j: (exp_made, ST_STEPS * b + j + 1),
            "pv": lambda b, j: (y_stored, 2 * b + j // 2 + 1),
            "y_turn": lambda b, j: (y_normed, TT * b + j + 1),
            "yn_turn": lambda b, j: (ynT_stored, b + 1),
            "proj": lambda b, j: (x1_made, b + 1),
            "ctx_qk": lambda b, j: (ctx_qk_made, 2 * (b + 1)),
            "ctx_scores": lambda b, j: (ctx_exped, TT * (b + 1)),
            "ctx_turn": lambda b, j: (attnT_stored, b + 1),
            "cross": lambda b, j: (x2_made, b + 1),
            "up": lambda b, j: (act_made, EP * b + j + 1),
            "gate": lambda b, j: (hidden_made, EP * b + j + 1),
            "down": lambda b, j: (result_made, TT * (b + 1)),
        }

        def free_bank(pe, name, b, j):
            former = BANK_BEFORE[name, b, j]
            if former is not None:
                pe.wait_ge(*FREED[former[0]](former[1], former[2]))
            return bank_of(name, b, j)

        block = ctx.enter_context(nc.Block())

        @block.sync
        def _(sp):
            def load(dst, src, signal):
                sp.dma_start(dst, src).then_inc(signal, 16)

            x_v = x_in.rearrange("b (i p) c -> p b i c", p=P)
            out_v = out.rearrange("b (i p) c -> p b i c", p=P)
            w_v = wqkvT_in.rearrange("(k p) n -> p k n", p=P)
            load(x[:, 0], x_v[:, 0], x_loaded[0])
            ctx_v = ctxT_in.rearrange("b c t -> c b t")
            load(w_ctx[:], wctxT_in.rearrange("a c d -> c a d"), ctx_loaded[0])
            load(ctxT[:, 0:2], ctx_v[:, 0:2], ctx_loaded[0])
            for m in range(CT):
                for s in range(2):
                    cols = slice(s * C + m * P, s * C + (m + 1) * P)
                    load(w_qkv[:, :, cols], w_v[:, :, cols], wqkv_loaded[m])
            load(x[:, 1], x_v[:, 1], x_loaded[1])
            load(ctxT[:, 2:4], ctx_v[:, 2:4], ctx_loaded[1])
            for j, (w, kt) in enumerate(((wupT_in, CT), (wgateT_in, CT), (wdownT_in, ET))):
                load(w_ffn[j][:].rearrange("p (k n) -> p k n", k=kt), w.rearrange("(k p) n -> p k n", p=P),
                     ffn_loaded[j])
            load(x[:, 2], x_v[:, 2], x_loaded[2])
            load(w_proj[:], wpT_in.rearrange("(k p) n -> p k n", p=P), wproj_loaded)
            load(x[:, 3], x_v[:, 3], x_loaded[3])
            for name, b, j in ORDER[SP]:
                if name in ("pack_hi", "pack_lo"):
                    a = 0 if name == "pack_hi" else 1
                    sp.wait_ge((qk_hi, qk_lo)[a], 2 * b + j + 1)
                    if b % 2 == 0:
                        sp.wait_ge(pads_set, 2 * j + 2)
                    if b >= 2:
                        sp.wait_ge(st_made, ST_STEPS * (b - 2) + ST_HALF * (j + 1))
                    heads = slice(j * HALF, (j + 1) * HALF)
                    both = pack[b % 2][3 * D * a:(3 * a + 1) * D, heads].rearrange("d h s t -> d h (s t)")
                    sp.dma_start(both.bitcast(F32), parts[j][:, a].rearrange("p s t -> p (s t)").bitcast(F32)
                                 ).then_inc(packed[j][b % 2], 16)
                    for s, t in ((0, 1 + a), (1, 2 - a)):
                        sp.dma_start(pack[b % 2][D * t:D * (t + 1), heads, s].bitcast(F32),
                                     parts[j][:, a, s].bitcast(F32)).then_inc(packed[j][b % 2], 16)
                elif name == "pad_copy":
                    sp.wait_ge(pads_set, 4)
                    sp.dma_start(pack[1][TERMS * D:MROW + MAX_PARTS].bitcast(F32),
                                 pack[0][TERMS * D:MROW + MAX_PARTS].bitcast(F32)).then_inc(pads_copied, 16)
                elif name == "max_rows":
                    sp.wait_ge(maxT_made, 2 * b + j + 1)
                    sp.wait_ge(pads_copied, 16)
                    if b >= 2:
                        sp.wait_ge(st_made, ST_STEPS * (b - 2) + ST_HALF * (j + 1))
                    sp.dma_start(pack[b % 2][MROW:MROW + 2, j * HALF:(j + 1) * HALF, 0].bitcast(F32),
                                 maxT[j][:]).then_inc(max_placed[j][b % 2], 16)
                elif name == "store":
                    sp.wait_ge(result_made, TT * b + j + 1)
                    sp.dma_start(out_v[:, b, j], result[:, j]).then_inc(stored[j], 16)
            for j in range(TT):
                sp.wait_ge(stored[j], 16 * B)

        @block.gpsimd
        def _(pool):
            nc.gpsimd.memset(neg_half[:], -0.5).then_inc(neg_half_set, 1)
            nc.gpsimd.memset(mask16[:], MASKED).then_inc(mask_filled, 1)
            pool.wait_ge(mask_filled, 1)
            nc.gpsimd.affine_select(out=mask16[:], in_=mask16[:], compare_op=ALU.is_gt, fill=0.0, base=0,
                                    pattern=[[0, 4], [1, P]], channel_multiplier=-1).then_inc(mask_made, 1)
            pool.wait_ge(mask_made, 1)
            for i in range(2):
                if i:
                    pool.wait_ge(v_ones_set, 1)
                nc.gpsimd.memset(v_aug[i][:, :, :, D:32], 1.0).then_inc(v_ones_set, 1)
            pool.wait_ge(v_ones_set, 2)
            for name, b, j in ORDER[POOL]:
                if name.startswith("rstd"):
                    k = int(name[-1]) - 1
                    pool.wait_ge(var_made[k], b + 1)
                    pool.wait_ge(neg_half_set, 1)
                    if b:
                        pool.wait_ge(normed[k], TT * b)
                    nc.gpsimd.tensor_tensor(rstd[k][:], var_eps[k][:], neg_half[:], ALU.pow).then_inc(rstd_made[k], 1)
                    pool.wait_ge(rstd_made[k], b + 1)
                    pool.wait_ge(neg_mean_made[k], b + 1)
                    nc.gpsimd.tensor_tensor(ln_bias[k][:], neg_mean[k][:], rstd[k][:], ALU.mult
                                            ).then_inc(ln_bias_made[k], 1)
                elif name == "pad":
                    m, s = j // 2, j % 2
                    nc.gpsimd.memset(pack[0][:, m * HALF:(m + 1) * HALF, s].bitcast(F32), float(s)
                                     ).then_inc(pads_set, 1)
                elif name == "rotate_add":
                    n = 2 * b + j
                    pool.wait_ge(qk_swapped, n + 1)
                    nc.gpsimd.tensor_tensor(swapped[j][:], swapped[j][:],
                                            sin_t.rearrange("p (k t) -> p k t", k=1).broadcast_to((P, CT, T)),
                                            ALU.mult).then_inc(qk_sin, 1)
                    pool.wait_ge(qk_sin, n + 1)
                    pool.wait_ge(qk_cos, n + 1)
                    nc.gpsimd.tensor_tensor(turned[j][:], turned[j][:], swapped[j][:], ALU.add).then_inc(qk_rotated, 1)
                elif name == "qk_lo":
                    pool.wait_ge(qk_hi, 2 * b + j + 1)
                    if b:
                        pool.wait_ge(packed[j][(b - 1) % 2], 16 * PACK_DMAS * ((b - 1) // 2 + 1))
                    nc.gpsimd.tensor_tensor(parts[j][:, 1], turned[j][:], parts[j][:, 0].bitcast(F32), ALU.subtract
                                            ).then_inc(qk_lo, 1)
                elif name == "mask":
                    n = G * b + j
                    pr = probs[n % 2]
                    pool.wait_ge(exp_made, 3 * (n + 1))
                    for sel in (pr[:, 0:2, :].rearrange("p u (h q) -> p (u h) q", q=T)[:, :, 0:P],
                                pr[:, 2, :].rearrange("p (h q) -> p h q", q=P)):
                        nc.gpsimd.affine_select(out=sel, in_=sel, compare_op=ALU.is_ge, fill=0.0, base=0,
                                                pattern=[[0, 4], [1, P]], channel_multiplier=-1
                                                ).then_inc(probs_masked, 1)
                elif name == "hid_lo":
                    n = EP * b + j
                    pool.wait_ge(hid_hi, n + 1)
                    nc.gpsimd.tensor_tensor(hid[:, 1, 2 * j:2 * j + 2], pair[n % RING], hid[:, 0, 2 * j:2 * j + 2],
                                            ALU.subtract).then_inc(hid_lo, 1)

        @block.scalar
        def _(act):
            act.dma_start(b_ctx[:], bctx_in).then_inc(ctx_loaded[0], 16)
            act.dma_start(consts[:], consts_in).then_inc(consts_loaded, 16)
            act.dma_start(w_qkv[:, :, 2 * C:], wqkvT_in.rearrange("(k p) n -> p k n", p=P)[:, :, 2 * C:]
                          ).then_inc(wqkv_loaded[2], 16)
            for name, b, j in ORDER[ACTE]:
                if name == "w_hi":
                    act.wait_ge(wqkv_loaded[j], 32 if j < CT else 16)
                    nc.scalar.activation(w_third(w_qkv_hi, j), w_third(w_qkv, j), ACT.Copy).then_inc(w_hi_made, 1)
                elif name == "abs":
                    act.wait_ge(ffn_loaded[j], 16)
                    if j:
                        act.wait_ge(abs_summed, j)
                    nc.scalar.activation(tern_neg[:], w_ffn[j][:], ACT.Abs, accum_out=abs_sum[:, j:j + 1]
                                         ).then_inc(abs_summed, 1)
                elif name.startswith("apply"):
                    k = int(name[-1]) - 1
                    act.wait_ge(ln_bias_made[k], b + 1)
                    if b:
                        act.wait_ge(turned_ln[k], b)
                    if k == 2:
                        act.wait_ge(tern_made, 3)
                    for i in range(TT):
                        nc.scalar.activation(xn[k][:, i], x[:, b, i], ACT.Identity, bias=ln_bias[k][:, i:i + 1],
                                             scale=rstd[k][:, i:i + 1]).then_inc(normed[k], 1)
                elif name == "ln_hi1":
                    act.wait_ge(turned_ln[0], b + 1)
                    if b:
                        act.wait_ge(v_projected, b)
                        act.wait_ge(qk_projected, 2 * b)
                        act.wait_ge(lnT_lo[0], b)
                    nc.scalar.activation(xT_hi[:], bank_of("ln_turn1", b, 0)[:].rearrange("p (k t) -> p k t", k=CT),
                                         ACT.Copy).then_inc(lnT_hi[0], 1)
                elif name == "ln_hi2":
                    act.wait_ge(turned_ln[1], b + 1)
                    if b:
                        act.wait_ge(crossed, b)
                    nc.scalar.activation(x2T[:], bank_of("ln_turn2", b, 0)[:].rearrange("p (k t) -> p k t", k=CT),
                                         ACT.Copy).then_inc(lnT_hi[1], 1)
                elif name == "ln_hi3":
                    act.wait_ge(turned_ln[2], b + 1)
                    act.wait_ge(tern_made, 3)
                    if b:
                        act.wait_ge(gate_made, EP * b)
                        act.wait_ge(lnT_lo[2], b)
                    nc.scalar.activation(x3T[:, 0], bank_of("ln_turn3", b, 0)[:].rearrange("p (k t) -> p k t", k=CT),
                                         ACT.Copy).then_inc(lnT_hi[2], 1)
                elif name == "qk_hi":
                    act.wait_ge(qk_rotated, 2 * b + j + 1)
                    if b:
                        act.wait_ge(packed[j][(b - 1) % 2], 16 * PACK_DMAS * ((b - 1) // 2 + 1))
                    nc.scalar.activation(parts[j][:, 0], turned[j][:], ACT.Copy).then_inc(qk_hi, 1)
                elif name == "v_store":
                    act.wait_ge(v_projected, b + 1)
                    act.wait_ge(v_ones_set, 2)
                    if b >= 2:
                        act.wait_ge(pv_made, G * (b - 1))
                    nc.scalar.activation(v_aug[b % 2][:, :, :, 0:D],
                                         bank_of("v", b, 0)[:].rearrange("p (k h d) -> p k h d", k=TT, h=H), ACT.Copy
                                         ).then_inc(v_stored, 1)
                elif name == "max_store":
                    act.wait_ge(max_turned, 2 * b + j + 1)
                    if b:
                        act.wait_ge(max_placed[j][(b - 1) % 2], 16 * ((b - 1) // 2 + 1))
                    nc.scalar.activation(maxT[j][:], bank_of("max_turn", b, j)[0:2 * HALF, 0:T], ACT.Copy
                                         ).then_inc(maxT_made, 1)
                elif name == "exp":
                    n = ST_STEPS * b + j
                    g = n // 3
                    act.wait_ge(st_made, n + 1)
                    if g >= 2:
                        act.wait_ge(pv_made, g - 1)
                    nc.scalar.activation(probs[g % 2][:, j % 3, :], bank_of("st", b, j)[:], ACT.Exp, scale=D ** -0.5
                                         ).then_inc(exp_made, 1)
                elif name == "y_store":
                    act.wait_ge(pv_made, G * b + 2 * j + 2)
                    act.wait_ge(w_lo_made, 3)
                    if b:
                        act.wait_ge(y_turned, TT * b)
                    nc.scalar.activation(yT_raw[:, 2 * j:2 * j + 2, :],
                                         bank_of("pv", b, 2 * j)[:].rearrange("p (g t) -> p g t", g=2), ACT.Copy
                                         ).then_inc(y_stored, 1)
                elif name == "yn_store":
                    act.wait_ge(yn_turned, b + 1)
                    if b:
                        act.wait_ge(projected, b)
                    nc.scalar.activation(ynT[:], bank_of("yn_turn", b, 0)[:].rearrange("p (k t) -> p k t", k=CT),
                                         ACT.Copy).then_inc(ynT_stored, 1)
                elif name == "ctx_bias":
                    act.wait_ge(ctx_projected, b + 1)
                    act.wait_ge(ctx_loaded[0], 48)
                    if b:
                        act.wait_ge(ctx_scored, b)
                    for a in range(2):
                        nc.scalar.activation(ctx_qk[:, a], bank_of("ctx_qk", b, 0)[:, a * T:(a + 1) * T],
                                             ACT.Identity, bias=b_ctx[:, a:a + 1]).then_inc(ctx_qk_made, 1)
                elif name == "ctx_exp":
                    act.wait_ge(ctx_maxed, b + 1)
                    if b:
                        act.wait_ge(ctx_normed, TT * b)
                    for i in range(TT):
                        nc.scalar.activation(ctx_exp[:, i], bank_of("ctx_scores", b, 0)[:, i * T:(i + 1) * T],
                                             ACT.Exp, bias=ctx_negmax[:, i:i + 1], accum_out=ctx_sum[:, i:i + 1]
                                             ).then_inc(ctx_exped, 1)
                elif name == "ctx_store":
                    act.wait_ge(ctx_turned, b + 1)
                    if b >= 2:
                        act.wait_ge(crossed, b - 1)
                    nc.scalar.activation(attnT[b % 2][:], bank_of("ctx_turn", b, 0)[:].rearrange(
                        "p (k t) -> p k t", k=CT), ACT.Copy).then_inc(attnT_stored, 1)
                elif name == "tanh":
                    n = EP * b + j
                    act.wait_ge(up_made, n + 1)
                    act.wait_ge(halves_made, 2)
                    act.wait_ge(tern_made, 2)
                    if n >= RING:
                        act.wait_ge(hid_hi, n - RING + 1)
                        act.wait_ge(hid_lo, n - RING + 1)
                    nc.scalar.activation(pair[n % RING], bank_of("up", b, j)[:].rearrange("p (m t) -> p m t", m=2),
                                         ACT.Tanh, scale=half_pos[:, 0:1]).then_inc(tanh_made, 1)
                elif name == "hid_hi":
                    n = EP * b + j
                    act.wait_ge(hidden_made, n + 1)
                    if b:
                        act.wait_ge(down_made, EP * (b - 1) + j + 1)
                    nc.scalar.activation(hid[:, 0, 2 * j:2 * j + 2], pair[n % RING], ACT.Copy).then_inc(hid_hi, 1)

        @block.vector
        def _(dve):
            nc.vector.memset(ones[:], 1.0).then_inc(ones_set, 1)
            for name, b, j in ORDER[DVE]:
                if name == "scales":
                    dve.wait_ge(abs_total, 1)
                    nc.vector.tensor_scalar(scales[:], bank_of("abs_total", 0, 0)[:, 0:3], 1.0 / (C * E), EPS_Q,
                                            ALU.mult, ALU.add).then_inc(scales_made, 1)
                    dve.wait_ge(scales_made, 1)
                    nc.vector.tensor_scalar(half_pos[:], scales[:], 0.5, None, ALU.mult).then_inc(halves_made, 1)
                    nc.vector.tensor_scalar(half_neg[:], scales[:], -0.5, None, ALU.mult).then_inc(halves_made, 1)
                    nc.vector.tensor_tensor(out_scale[:, 0:1], scales[:, 0:1], scales[:, 1:2], ALU.mult
                                            ).then_inc(out_scale_made, 1)
                    dve.wait_ge(out_scale_made, 1)
                    nc.vector.tensor_scalar(out_scale[:, 1:2], out_scale[:, 0:1], scales[:, 2:3], 4.0, ALU.mult,
                                            ALU.mult).then_inc(out_scale_made, 1)
                elif name == "below":
                    dve.wait_ge(halves_made, 2)
                    dve.wait_ge(abs_summed, 3)
                    if j:
                        dve.wait_ge(tern_made, j)
                    nc.vector.tensor_scalar(tern_neg[:], w_ffn[j][:], half_neg[:, j:j + 1], None, ALU.is_lt
                                            ).then_inc(below_made, 1)
                elif name == "ternary":
                    dve.wait_ge(below_made, j + 1)
                    nc.vector.scalar_tensor_tensor(w_tern[j][:], w_ffn[j][:], half_pos[:, j:j + 1], tern_neg[:],
                                                   ALU.is_gt, ALU.subtract).then_inc(tern_made, 1)
                elif name == "w_lo":
                    dve.wait_ge(w_hi_made, j + 1)
                    nc.vector.tensor_tensor(w_third(w_qkv_lo, j), w_third(w_qkv, j), w_third(w_qkv_hi, j).bitcast(F32),
                                            ALU.subtract).then_inc(w_lo_made, 1)
                    if j == 0:
                        dve.wait_ge(consts_loaded, 16)
                        nc.vector.tensor_copy(ident16[:], ident).then_inc(ident16_made, 1)
                elif name.startswith("stats"):
                    k = int(name[-1]) - 1
                    dve.wait_ge(*((x_loaded[b], 16), (x1_made, b + 1), (x2_made, b + 1))[k])
                    for i in range(TT):
                        nc.vector.bn_stats(stats[k][:, i], x[:, b, i]).then_inc(stats_made[k], 1)
                    dve.wait_ge(stats_made[k], TT * (b + 1))
                    for i in range(TT):
                        nc.vector.bn_aggr(mean_var[k][:, i], stats[k][:, i]).then_inc(moments_made[k], 1)
                    dve.wait_ge(moments_made[k], TT * (b + 1))
                    if b:
                        dve.wait_ge(ln_bias_made[k], b)
                    nc.vector.tensor_scalar(var_eps[k][:], mean_var[k][:, :, 1], EPS_LN, None, ALU.add
                                            ).then_inc(var_made[k], 1)
                    nc.vector.tensor_scalar(neg_mean[k][:], mean_var[k][:, :, 0], -1.0, None, ALU.mult
                                            ).then_inc(neg_mean_made[k], 1)
                elif name == "ln_lo1":
                    dve.wait_ge(lnT_hi[0], b + 1)
                    nc.vector.tensor_tensor(xT_lo[:], bank_of("ln_turn1", b, 0)[:].rearrange("p (k t) -> p k t", k=CT),
                                            xT_hi[:].bitcast(F32), ALU.subtract).then_inc(lnT_lo[0], 1)
                elif name == "ln_lo3":
                    dve.wait_ge(lnT_hi[2], b + 1)
                    nc.vector.tensor_tensor(x3T[:, 1], bank_of("ln_turn3", b, 0)[:].rearrange("p (k t) -> p k t", k=CT),
                                            x3T[:, 0], ALU.subtract).then_inc(lnT_lo[2], 1)
                elif name == "rotate":
                    n = 2 * b + j
                    bank = bank_of("qk", b, j)
                    dve.wait_ge(qk_projected, n + 1)
                    if b:
                        dve.wait_ge(qk_rotated, n - 1)
                        dve.wait_ge(qk_hi, n - 1)
                        dve.wait_ge(qk_lo, n - 1)
                    nc.vector.stream_shuffle(swapped[j][:].rearrange("p k t -> p (k t)"), bank[:],
                                             [i ^ HALF for i in range(32)]).then_inc(qk_swapped, 1)
                    nc.vector.tensor_tensor(turned[j][:], bank[:].rearrange("p (k t) -> p k t", k=CT),
                                            cos_t.rearrange("p (k t) -> p k t", k=1).broadcast_to((P, CT, T)),
                                            ALU.mult).then_inc(qk_cos, 1)
                elif name == "sq_max":
                    dve.wait_ge(sq_made, SQ_STEPS * b + j + 1)
                    m, u = j // SQ_HALF, j % SQ_HALF
                    if u == 0 and b:
                        dve.wait_ge(max_lo, 2 * (b - 1) + m + 1)
                    if u < 2:
                        into, heads = neg_max[m][:, 0, 4 * u:4 * u + 4], 4
                    else:
                        into, heads = neg_max[m][:, 1, 2 * (u - 2):2 * (u - 2) + 2], 2
                    nc.vector.tensor_reduce(into, bank_of("sq", b, j)[:].rearrange("p (h k) -> p h k", h=heads), AX.X,
                                            ALU.max, negate=True).then_inc(sq_maxed, 1)
                elif name == "max_split":
                    dve.wait_ge(sq_maxed, SQ_STEPS * b + SQ_HALF * (j + 1))
                    if b:
                        dve.wait_ge(max_turned, 2 * (b - 1) + j + 1)
                    nc.vector.tensor_copy(max_parts[j][:, :, 0], neg_max[j][:]).then_inc(max_hi, 1)
                    dve.wait_ge(max_hi, 2 * b + j + 1)
                    nc.vector.tensor_tensor(max_parts[j][:, :, 1], neg_max[j][:], max_parts[j][:, :, 0].bitcast(F32),
                                            ALU.subtract).then_inc(max_lo, 1)
                elif name == "y_norm":
                    n = TT * b + j
                    dve.wait_ge(y_turned, n + 1)
                    dve.wait_ge(w_lo_made, 3)
                    if b:
                        dve.wait_ge(yn_turned, b)
                    bank = bank_of("y_turn", b, j)[:].rearrange("p (h d) -> p h d", d=32)
                    nc.vector.reciprocal(y_rec[:, j].rearrange("p (h a) -> p h a", a=1), bank[:, :, D:D + 1]
                                         ).then_inc(y_rec_made, 1)
                    dve.wait_ge(y_rec_made, n + 1)
                    nc.vector.tensor_tensor(yn[:, j].rearrange("p (h d) -> p h d", d=D), bank[:, :, 0:D],
                                            y_rec[:, j].rearrange("p (h a) -> p h a", a=1).broadcast_to((P, H, D)),
                                            ALU.mult).then_inc(y_normed, 1)
                elif name == "add1":
                    dve.wait_ge(projected, b + 1)
                    nc.vector.tensor_tensor(x[:, b], bank_of("proj", b, 0)[:].rearrange("p (i c) -> p i c", i=TT),
                                            x[:, b], ALU.add).then_inc(x1_made, 1)
                elif name == "add2":
                    dve.wait_ge(crossed, b + 1)
                    nc.vector.tensor_tensor(x[:, b], bank_of("cross", b, 0)[:].rearrange("p (i c) -> p i c", i=TT),
                                            x[:, b], ALU.add).then_inc(x2_made, 1)
                elif name == "ctx_max":
                    dve.wait_ge(ctx_scored, b + 1)
                    if b:
                        dve.wait_ge(ctx_exped, TT * b)
                    nc.vector.tensor_reduce(ctx_negmax[:], bank_of("ctx_scores", b, 0)[:].rearrange(
                        "p (i n) -> p i n", i=TT), AX.X, ALU.max, negate=True).then_inc(ctx_maxed, 1)
                elif name == "ctx_norm":
                    dve.wait_ge(ctx_exped, TT * (b + 1))
                    if b:
                        dve.wait_ge(ctx_turned, b)
                    nc.vector.reciprocal(ctx_rec[:], ctx_sum[:]).then_inc(ctx_rec_made, 1)
                    dve.wait_ge(ctx_rec_made, b + 1)
                    for i in range(TT):
                        nc.vector.tensor_scalar(ctx_attn[:, i], ctx_exp[:, i], ctx_rec[:, i:i + 1], None, ALU.mult
                                                ).then_inc(ctx_normed, 1)
                elif name == "act":
                    n = EP * b + j
                    dve.wait_ge(tanh_made, n + 1)
                    nc.vector.scalar_tensor_tensor(pair[n % RING], pair[n % RING], 1.0,
                                                   bank_of("up", b, j)[:].rearrange("p (m t) -> p m t", m=2),
                                                   ALU.add, ALU.mult).then_inc(act_made, 1)
                elif name == "hidden":
                    n = EP * b + j
                    dve.wait_ge(gate_made, n + 1)
                    dve.wait_ge(act_made, n + 1)
                    nc.vector.scalar_tensor_tensor(pair[n % RING],
                                                   bank_of("gate", b, j)[:].rearrange("p (m t) -> p m t", m=2), 0.125,
                                                   pair[n % RING], ALU.mult, ALU.mult).then_inc(hidden_made, 1)
                elif name == "result":
                    dve.wait_ge(down_made, EP * (b + 1))
                    dve.wait_ge(out_scale_made, 2)
                    dve.wait_ge(tern_made, 2)
                    if b:
                        dve.wait_ge(stored[j], 16 * b)
                    nc.vector.scalar_tensor_tensor(result[:, j], bank_of("down", b, 0)[:, j * C:(j + 1) * C],
                                                   out_scale[:, 1:2], x[:, b, j], ALU.mult, ALU.add
                                                   ).then_inc(result_made, 1)

        @block.tensor
        def _(pe):
            def turn(dst, src, signal):
                for i in range(TT):
                    for k in range(CT):
                        last = nc.tensor.transpose(dst[:, k * T + i * P:k * T + (i + 1) * P],
                                                   src[:, i, k * P:(k + 1) * P], ident)
                last.then_inc(signal, 1)

            pe.wait_ge(ones_set, 1)
            for _ in range(WARM_UP):
                nc.tensor.matmul(banks[-1][:, 0:P], ones[:], ones[:], start=True, stop=True)
            for name, b, j in ORDER[PE]:
                bank = free_bank(pe, name, b, j) if j % SHARED.get(name, 1) == 0 else bank_of(name, b, j)
                if name == "abs_total":
                    pe.wait_ge(ones_set, 1)
                    pe.wait_ge(abs_summed, 3)
                    nc.tensor.matmul(bank[:, 0:3], ones[:], abs_sum[:], start=True, stop=True
                                     ).then_inc(abs_total, 1)
                elif name.startswith("ln_turn"):
                    k = int(name[-1]) - 1
                    pe.wait_ge(normed[k], TT * (b + 1))
                    pe.wait_ge(consts_loaded, 16)
                    turn(bank, xn[k], turned_ln[k])
                elif name == "qk":
                    pe.wait_ge(lnT_lo[0], b + 1)
                    pe.wait_ge(w_lo_made, j + 1)
                    for s in range(2):
                        cols = slice(s * C + j * P, s * C + (j + 1) * P)
                        terms = [(k, w, a) for k in range(CT) for w, a in
                                 ((w_qkv_hi, xT_hi), (w_qkv_hi, xT_lo), (w_qkv_lo, xT_hi))]
                        for t, (k, w, a) in enumerate(terms):
                            last = nc.tensor.matmul(bank[:, s * T:(s + 1) * T], w[:, k, cols], a[:, k, :],
                                                    start=(t == 0), stop=(t == len(terms) - 1))
                    last.then_inc(qk_projected, 1)
                elif name == "v":
                    pe.wait_ge(lnT_lo[0], b + 1)
                    pe.wait_ge(w_lo_made, 3)
                    for i in range(TT):
                        terms = [(k, w, a) for k in range(CT) for w, a in
                                 ((w_qkv_hi, xT_hi), (w_qkv_hi, xT_lo), (w_qkv_lo, xT_hi))]
                        for t, (k, w, a) in enumerate(terms):
                            last = nc.tensor.matmul(bank[:, i * C:(i + 1) * C], a[:, k, i * P:(i + 1) * P],
                                                    w[:, k, 2 * C:3 * C], start=(t == 0), stop=(t == len(terms) - 1))
                    last.then_inc(v_projected, 1)
                elif name == "sq":
                    n = SQ_STEPS * b + j
                    q, k = pack[b % 2][:, :, 0], pack[b % 2][:, :, 1]
                    m, u = j // SQ_HALF, j % SQ_HALF
                    if u == 0:
                        pe.wait_ge(ident16_made, 1)
                        pe.wait_ge(mask_made, 1)
                        pe.wait_ge(packed[m][b % 2], 16 * PACK_DMAS * (b // 2 + 1))
                        if b % 2:
                            pe.wait_ge(pads_copied, 16)
                    if u < 2:
                        nc.tensor.matmul(bank[:], ident16[:], mask16[:].rearrange("p a k -> p (a k)"), start=True,
                                         stop=False, skip_group_check=True)
                        for a in range(4):
                            h = m * HALF + 4 * u + a
                            last = nc.tensor.matmul(bank[:, a * P:(a + 1) * P], q[0:MROW, h, 0:P], k[0:MROW, h, 0:P],
                                                    start=False, stop=(a == 3), skip_group_check=True)
                    else:
                        nc.tensor.matmul(bank[:].rearrange("p (h k) -> p h k", h=2)[:, :, P:T], ident16[:],
                                         mask16[:, 0:2, :], start=True, stop=False, skip_group_check=True)
                        for a in range(2):
                            h = m * HALF + 2 * (u - 2) + a
                            last = nc.tensor.matmul(bank[:, a * T:(a + 1) * T], q[0:MROW, h, P:T], k[0:MROW, h, :],
                                                    start=False, stop=(a == 1), skip_group_check=True)
                    last.then_inc(sq_made, 1)
                elif name == "max_turn":
                    pe.wait_ge(max_lo, 2 * b + j + 1)
                    for i in range(TT):
                        last = nc.tensor.transpose(bank[0:2 * HALF, i * P:(i + 1) * P],
                                                   max_parts[j][:, i].rearrange("p a h -> p (a h)").bitcast(F32),
                                                   ident)
                    last.then_inc(max_turned, 1)
                elif name == "st":
                    n = ST_STEPS * b + j
                    q, k = pack[b % 2][:, :, 0], pack[b % 2][:, :, 1]
                    if j % ST_HALF == 0:
                        pe.wait_ge(max_placed[j // ST_HALF][b % 2], 16 * (b // 2 + 1))
                    g, u = j // 3, j % 3
                    K = MROW + MAX_PARTS
                    if u < 2:
                        for a in range(2):
                            h = 4 * g + 2 * u + a
                            last = nc.tensor.matmul(bank[:, a * T:(a + 1) * T], k[0:K, h, 0:P], q[0:K, h, :],
                                                    start=True, stop=True)
                    else:
                        for a in range(4):
                            h = 4 * g + a
                            last = nc.tensor.matmul(bank[:, a * P:(a + 1) * P], k[0:K, h, P:T], q[0:K, h, P:T],
                                                    start=True, stop=True)
                    last.then_inc(st_made, 1)
                elif name == "pv":
                    n = G * b + j
                    pe.wait_ge(probs_masked, 2 * (n + 1))
                    if j == 0:
                        pe.wait_ge(v_stored, b + 1)
                    pr, va, off = probs[n % 2], v_aug[b % 2], (j % 2) * T
                    for a in range(4):
                        nc.tensor.matmul(bank[32 * a:32 * a + 32, off:off + T], va[:, 0, 4 * j + a, :],
                                         pr[:, a // 2, (a % 2) * T:(a % 2) * T + T], start=True, stop=False,
                                         skip_group_check=True)
                    for a in range(4):
                        last = nc.tensor.matmul(bank[32 * a:32 * a + 32, off + P:off + T], va[:, 1, 4 * j + a, :],
                                                pr[:, 2, a * P:(a + 1) * P], start=False, stop=True,
                                                skip_group_check=True)
                    last.then_inc(pv_made, 1)
                elif name == "y_turn":
                    pe.wait_ge(y_stored, 2 * (b + 1))
                    for g in range(G):
                        last = nc.tensor.transpose(bank[:, g * P:(g + 1) * P], yT_raw[:, g, j * P:(j + 1) * P],
                                                   ident)
                    last.then_inc(y_turned, 1)
                elif name == "yn_turn":
                    pe.wait_ge(y_normed, TT * (b + 1))
                    turn(bank, yn, yn_turned)
                elif name == "proj":
                    pe.wait_ge(ynT_stored, b + 1)
                    pe.wait_ge(wproj_loaded, 16)
                    for i in range(TT):
                        for k in range(CT):
                            last = nc.tensor.matmul(bank[:, i * C:(i + 1) * C], ynT[:, k, i * P:(i + 1) * P],
                                                    w_proj[:, k, :], start=(k == 0), stop=(k == CT - 1))
                    last.then_inc(projected, 1)
                elif name == "cross":
                    pe.wait_ge(lnT_hi[1], b + 1)
                    pe.wait_ge(attnT_stored, b + 1)
                    for i in range(TT):
                        for k in range(CT):
                            last = nc.tensor.matmul(bank[:, i * C:(i + 1) * C], x2T[:, k, i * P:(i + 1) * P],
                                                    attnT[b % 2][:, k, :], start=(k == 0), stop=(k == CT - 1))
                    last.then_inc(crossed, 1)
                elif name == "ctx_qk":
                    pe.wait_ge(ctx_loaded[0], 48)
                    if b >= 2:
                        pe.wait_ge(ctx_loaded[1], 16)
                    for a in range(2):
                        last = nc.tensor.matmul(bank[:, a * T:(a + 1) * T], w_ctx[:, a, :], ctxT[:, b, :],
                                                start=True, stop=True)
                    last.then_inc(ctx_projected, 1)
                elif name == "ctx_scores":
                    pe.wait_ge(ctx_qk_made, 2 * (b + 1))
                    for i in range(TT):
                        last = nc.tensor.matmul(bank[:, i * T:(i + 1) * T], ctx_qk[:, 0, i * P:(i + 1) * P],
                                                ctx_qk[:, 1, :], start=True, stop=True)
                    last.then_inc(ctx_scored, 1)
                elif name == "ctx_turn":
                    pe.wait_ge(ctx_normed, TT * (b + 1))
                    turn(bank, ctx_attn, ctx_turned)
                elif name in ("up", "gate"):
                    w = 0 if name == "up" else 1
                    pe.wait_ge(lnT_lo[2], b + 1)
                    pe.wait_ge(tern_made, w + 1)
                    wt = w_tern[w][:].rearrange("p (k n) -> p k n", k=CT)
                    for a in range(2):
                        m = 2 * j + a
                        for t in range(2 * CT):
                            last = nc.tensor.matmul(bank[:, a * T:(a + 1) * T], wt[:, t // 2, m * P:(m + 1) * P],
                                                    x3T[:, t % 2, t // 2, :], start=(t == 0), stop=(t == 2 * CT - 1))
                    last.then_inc((up_made, gate_made)[w], 1)
                elif name == "down":
                    pe.wait_ge(hid_lo, EP * b + j + 1)
                    pe.wait_ge(tern_made, 3)
                    wt = w_tern[2][:].rearrange("p (k n) -> p k n", k=ET)
                    for i in range(TT):
                        for k in range(2 * j, 2 * j + 2):
                            for a in range(2):
                                last = nc.tensor.matmul(bank[:, i * C:(i + 1) * C], hid[:, a, k, i * P:(i + 1) * P],
                                                        wt[:, k, :], start=(i + k + a == 0),
                                                        stop=(k == ET - 1 and a == 1), skip_group_check=True)
                    last.then_inc(down_made, 1)


def constants():
    theta = (1.0 / 10000.0 ** (np.arange(0, D, 2, dtype=np.float32) / np.float32(D))).astype(np.float32)
    angle = np.outer(np.arange(T, dtype=np.float32), theta).astype(np.float32)
    channel = np.arange(P) // HALF
    cos = np.cos(angle).astype(np.float32)[:, channel // 2].T
    sin = np.sin(angle).astype(np.float32)[:, channel // 2].T
    sin = sin * np.where(channel % 2 == 0, -1.0, 1.0).astype(np.float32)[:, None]
    return np.ascontiguousarray(np.concatenate([np.eye(P, dtype=np.float32), cos, sin], axis=1))


def kernel(**inputs):
    import concourse.bacc as bacc
    from concourse.bass_utils import run_bass_kernel_spmd

    a = {k: np.asarray(v) for k, v in inputs.items()}
    w_qkv = a["L0_attn_w_atten"]
    w_qk = w_qkv[:2 * C].reshape(2 * CT, HALF, D, C).transpose(0, 2, 1, 3).reshape(2 * C, C)
    arrays = {
        "x": a["x"],
        "ctxT": a["ctx_1024"].transpose(0, 2, 1),
        "wqkvT": np.concatenate([w_qk, w_qkv[2 * C:]]).T,
        "wpT": a["L0_attn_w_proj"].T,
        "wctxT": np.stack([a["L0_xattn_Wq"].T, a["L0_xattn_Wk"].T]),
        "bctx": np.stack([a["L0_xattn_bq"], a["L0_xattn_bk"]], axis=1),
        "wupT": a["L0_ffn_W_up"].T,
        "wgateT": a["L0_ffn_W_gate"].T,
        "wdownT": a["L0_ffn_W_down"].T,
        "consts": constants(),
    }
    arrays = {f"in_{k}": np.ascontiguousarray(v) for k, v in arrays.items()}
    nc = bacc.Bacc("TRN2", target_bir_lowering=False, num_devices=1)
    args = [nc.dram_tensor(k, v.shape, mybir.dt.from_np(v.dtype), kind="ExternalInput").ap() for k, v in arrays.items()]
    out = nc.dram_tensor("out", (B, T, C), F32, kind="ExternalOutput").ap()
    decoder_kernel(nc, *args, out)
    r = run_bass_kernel_spmd(nc, [arrays], core_ids=[0])
    return r.results[0]["out"]
```
